# Optimizing a Trainium2 kernel written in Bass

```python
import numpy as np
import jax
import jax.numpy as jnp

def _softmax(x, axis=-1):
    return jax.nn.softmax(x, axis=axis)

def _gelu(x):
    return jax.nn.gelu(x, approximate=True)

def _silu(x):
    return jax.nn.silu(x)

def _sigmoid(x):
    return jax.nn.sigmoid(x)

def _layernorm(x, axis=-1, eps=1e-05):
    m = jnp.mean(x, axis=axis, keepdims=True)
    v = jnp.var(x, axis=axis, keepdims=True)
    return (x - m) / jnp.sqrt(v + eps)

def _scatter_add(tgt, idx, src, axis=0):
    return tgt.at[idx].add(src)

def _segment_sum(src, seg, n):
    return jax.ops.segment_sum(src, seg, n)
kernel_name = 'mk_flamingo_gated_d2_seqx_r8_1d5e99'

def setup_inputs(seed: int=0):
    np.random.seed(seed)
    _w = jnp.asarray

    def _rec_inputs():
        import jax
        import jax.numpy as jnp
        _rk = jax.random.key(seed)
        x = -1.394e-06 + 0.9999 * jax.random.normal(jax.random.fold_in(_rk, 1), (64, 64, 128), jnp.float32)
        _lenS = 64 - jax.random.randint(jax.random.fold_in(_rk, 7), (64,), 0, max(1, 64 // 4) + 1, jnp.int32)
        _lenS2 = 64 - jax.random.randint(jax.random.fold_in(_rk, 8), (64,), 0, max(1, 64 // 4) + 1, jnp.int32)
        _ctx_1024P = jax.random.normal(jax.random.fold_in(_rk, 11), (64, 16, 128), jnp.float32)
        _ctx_1024c = jax.random.dirichlet(jax.random.fold_in(_rk, 511), 0.3 * jnp.ones((16,), jnp.float32), (64, 64))
        _ctx_1024t = jnp.einsum('bsk,bkd->bsd', _ctx_1024c, _ctx_1024P)
        _ctx_1024t = _ctx_1024t * jax.lax.rsqrt(jnp.mean(jnp.square(_ctx_1024t)) + 1e-12) * 0.953939
        ctx_1024 = -0.000392918 + 0.999932 * (_ctx_1024t + 0.3 * jax.random.normal(jax.random.fold_in(_rk, 611), (64, 64, 128), jnp.float32))
        _validS = jnp.arange(64)[None, :] < _lenS[:, None]
        _validS2 = jnp.arange(64)[None, :] < _lenS2[:, None]
        _causal = jnp.tril(jnp.ones((64, 64), dtype=bool))
        mask_BxS2_bk0 = jnp.logical_not(jnp.broadcast_to(_validS2[:, :], (64, 64)))
        _g = jax.random.normal(jax.random.fold_in(_rk, 9001), (2, 2), jnp.float32)
        _g = jnp.sign(_g) * jnp.maximum(jnp.abs(_g), 1.0) + (_g == 0) * 1.0
        g_xattn = _g[0]
        g_ffn = _g[1]
        return (x, ctx_1024, mask_BxS2_bk0, g_xattn, g_ffn)
    x, ctx_1024, mask_BxS2_bk0, g_xattn, g_ffn = _rec_inputs()

    def _L0_xattn_setup():
        import jax, jax.numpy as jnp
        import numpy as np
        DIM = 128
        DIM_LATENT = 128
        DIM_HEAD = 64
        INNER = max(DIM, DIM_LATENT)
        HEADS = INNER // DIM_HEAD
        SCALE = DIM_HEAD ** (-0.5)
        LN_EPS = 1e-05
        RMS_EPS = 1e-08

        def layernorm(x, g, b):
            mu = jnp.mean(x, axis=-1, keepdims=True)
            var = jnp.mean(jnp.square(x - mu), axis=-1, keepdims=True)
            return (x - mu) * jax.lax.rsqrt(var + LN_EPS) * g + b

        def rmsnorm(x, gamma):
            n = jnp.linalg.norm(x, axis=-1, keepdims=True) * x.shape[-1] ** (-0.5)
            return x / jnp.maximum(n, RMS_EPS) * gamma
        key = jax.random.key(seed)
        ks = jax.random.split(key, 8)
        b, n, nl = (8, 256, 64)
        x = jax.random.normal(ks[0], (b, n, DIM), dtype=jnp.float32)
        latents = jax.random.normal(ks[1], (b, nl, DIM_LATENT), dtype=jnp.float32)
        mask = jax.random.randint(ks[2], (b, n), 0, 2).astype(bool)
        init = lambda k, shape, fan_in: jax.random.normal(k, shape, jnp.float32) * fan_in ** (-0.5)
        return {'x': x, 'latents': latents, 'mask': mask, 'ln_x_g': jnp.ones((DIM,), jnp.float32), 'ln_x_b': jnp.zeros((DIM,), jnp.float32), 'ln_l_g': jnp.ones((DIM_LATENT,), jnp.float32), 'ln_l_b': jnp.zeros((DIM_LATENT,), jnp.float32), 'q_gamma': jnp.ones((DIM_HEAD,), jnp.float32), 'k_gamma': jnp.ones((DIM_HEAD,), jnp.float32), 'W_q': init(ks[3], (DIM_LATENT, INNER), DIM_LATENT), 'W_kv': init(ks[4], (DIM, 2 * INNER), DIM), 'W_out': init(ks[5], (INNER, DIM_LATENT), INNER), 'b_out': jnp.zeros((DIM_LATENT,), jnp.float32)}
    _L0_xattn_all = _L0_xattn_setup()
    _L0_xattn_in = {k: v for k, v in _L0_xattn_all.items() if k in ('ln_x_g', 'ln_x_b', 'ln_l_g', 'ln_l_b', 'q_gamma', 'k_gamma', 'W_q', 'W_kv', 'W_out', 'b_out')}
    del _L0_xattn_all

    def _L0_ffn_setup():
        import jax, jax.numpy as jnp
        import numpy as np
        B, N, D = (4, 512, 128)
        E, S, F = (16, 64, 256)
        DO = 128
        EPS = 1e-05

        def _layernorm(x, g, b):
            mu = jnp.mean(x, axis=-1, keepdims=True)
            var = jnp.mean(jnp.square(x - mu), axis=-1, keepdims=True)
            return (x - mu) * jax.lax.rsqrt(var + EPS) * g + b
        key = jax.random.key(seed)
        ks = jax.random.split(key, 8)
        d = {'x': jax.random.normal(ks[0], (B, N, D), dtype=jnp.float32), 'norm_g': jnp.ones((D,), jnp.float32), 'norm_b': jnp.zeros((D,), jnp.float32), 'slot_g': jnp.ones((D,), jnp.float32), 'slot_b': jnp.zeros((D,), jnp.float32), 'scale': jnp.ones((1,), jnp.float32), 'slot_embeds': jax.random.normal(ks[1], (E, S, D), jnp.float32) / np.sqrt(D), 'Wg': jax.random.normal(ks[2], (E, D, F), jnp.float32) * np.sqrt(2.0 / (D + F)), 'bg': jnp.zeros((E, F), jnp.float32), 'Wu': jax.random.normal(ks[3], (E, D, F), jnp.float32) * np.sqrt(2.0 / (D + F)), 'bu': jnp.zeros((E, F), jnp.float32), 'Wd': jax.random.normal(ks[4], (E, F, DO), jnp.float32) * np.sqrt(2.0 / (F + DO)), 'bd': jnp.zeros((E, DO), jnp.float32)}
        return d
    _L0_ffn_all = _L0_ffn_setup()
    _L0_ffn_in = {k: v for k, v in _L0_ffn_all.items() if k in ('norm_g', 'norm_b', 'slot_g', 'slot_b', 'scale', 'slot_embeds', 'Wg', 'bg', 'Wu', 'bu', 'Wd', 'bd')}
    del _L0_ffn_all

    def _L1_xattn_setup():
        import jax, jax.numpy as jnp
        import numpy as np
        B, M, N, DIM, DH, H = (8, 512, 64, 128, 128, 8)
        INNER = DH * H
        EPS = 1e-05

        def _layernorm(x, g, b):
            mu = jnp.mean(x, axis=-1, keepdims=True)
            var = jnp.var(x, axis=-1, keepdims=True)
            return (x - mu) * jax.lax.rsqrt(var + EPS) * g + b
        key = jax.random.key(seed)
        ks = jax.random.split(key, 8)
        sd = 0.02
        return {'x': jax.random.normal(ks[0], (B, M, DIM), jnp.float32), 'latents': jax.random.normal(ks[1], (B, N, DIM), jnp.float32), 'gamma_media': jnp.ones((DIM,), jnp.float32), 'beta_media': jnp.zeros((DIM,), jnp.float32), 'gamma_lat': jnp.ones((DIM,), jnp.float32), 'beta_lat': jnp.zeros((DIM,), jnp.float32), 'Wq': jax.random.normal(ks[2], (DIM, INNER), jnp.float32) * sd, 'bq': jnp.zeros((INNER,), jnp.float32), 'Wkv': jax.random.normal(ks[3], (DIM, 2 * INNER), jnp.float32) * sd, 'bkv': jnp.zeros((2 * INNER,), jnp.float32), 'Wo': jax.random.normal(ks[4], (INNER, DIM), jnp.float32) * sd, 'bo': jnp.zeros((DIM,), jnp.float32)}
    _L1_xattn_all = _L1_xattn_setup()
    _L1_xattn_in = {k: v for k, v in _L1_xattn_all.items() if k in ('gamma_media', 'beta_media', 'gamma_lat', 'beta_lat', 'Wq', 'bq', 'Wkv', 'bkv', 'Wo', 'bo')}
    del _L1_xattn_all

    def _L1_ffn_setup():
        import jax, jax.numpy as jnp
        import numpy as np
        from jax import lax
        DIM = 128
        HID = 256
        E = 8
        K = 2
        B, T = (2, 64)
        key = jax.random.key(seed)
        ks = jax.random.split(key, 5)
        scale = 1.0 / np.sqrt(DIM)
        x = jax.random.normal(ks[0], (B, T, DIM), dtype=jnp.float32)
        router_w = jax.random.normal(ks[1], (E, DIM), dtype=jnp.float32) * scale
        w_gate = jax.random.normal(ks[2], (E, HID, DIM), dtype=jnp.float32) * scale
        w_up = jax.random.normal(ks[3], (E, HID, DIM), dtype=jnp.float32) * scale
        w_down = jax.random.normal(ks[4], (E, DIM, HID), dtype=jnp.float32) * (1.0 / np.sqrt(HID))
        return {'x': x, 'router_w': router_w, 'w_gate': w_gate, 'w_up': w_up, 'w_down': w_down}
    _L1_ffn_all = _L1_ffn_setup()
    _L1_ffn_in = {k: v for k, v in _L1_ffn_all.items() if k in ('router_w', 'w_gate', 'w_up', 'w_down')}
    del _L1_ffn_all
    return {'x': x, 'ctx_1024': ctx_1024, 'mask_BxS2_bk0': mask_BxS2_bk0, 'g_xattn': g_xattn, 'g_ffn': g_ffn, 'L0_xattn_ln_x_g': _L0_xattn_in['ln_x_g'], 'L0_xattn_ln_x_b': _L0_xattn_in['ln_x_b'], 'L0_xattn_ln_l_g': _L0_xattn_in['ln_l_g'], 'L0_xattn_ln_l_b': _L0_xattn_in['ln_l_b'], 'L0_xattn_q_gamma': _L0_xattn_in['q_gamma'], 'L0_xattn_k_gamma': _L0_xattn_in['k_gamma'], 'L0_xattn_W_q': _L0_xattn_in['W_q'], 'L0_xattn_W_kv': _L0_xattn_in['W_kv'], 'L0_xattn_W_out': _L0_xattn_in['W_out'], 'L0_xattn_b_out': _L0_xattn_in['b_out'], 'L0_ffn_norm_g': _L0_ffn_in['norm_g'], 'L0_ffn_norm_b': _L0_ffn_in['norm_b'], 'L0_ffn_slot_g': _L0_ffn_in['slot_g'], 'L0_ffn_slot_b': _L0_ffn_in['slot_b'], 'L0_ffn_scale': _L0_ffn_in['scale'], 'L0_ffn_slot_embeds': _L0_ffn_in['slot_embeds'], 'L0_ffn_Wg': _L0_ffn_in['Wg'], 'L0_ffn_bg': _L0_ffn_in['bg'], 'L0_ffn_Wu': _L0_ffn_in['Wu'], 'L0_ffn_bu': _L0_ffn_in['bu'], 'L0_ffn_Wd': _L0_ffn_in['Wd'], 'L0_ffn_bd': _L0_ffn_in['bd'], 'L1_xattn_gamma_media': _L1_xattn_in['gamma_media'], 'L1_xattn_beta_media': _L1_xattn_in['beta_media'], 'L1_xattn_gamma_lat': _L1_xattn_in['gamma_lat'], 'L1_xattn_beta_lat': _L1_xattn_in['beta_lat'], 'L1_xattn_Wq': _L1_xattn_in['Wq'], 'L1_xattn_bq': _L1_xattn_in['bq'], 'L1_xattn_Wkv': _L1_xattn_in['Wkv'], 'L1_xattn_bkv': _L1_xattn_in['bkv'], 'L1_xattn_Wo': _L1_xattn_in['Wo'], 'L1_xattn_bo': _L1_xattn_in['bo'], 'L1_ffn_router_w': _L1_ffn_in['router_w'], 'L1_ffn_w_gate': _L1_ffn_in['w_gate'], 'L1_ffn_w_up': _L1_ffn_in['w_up'], 'L1_ffn_w_down': _L1_ffn_in['w_down']}

def reference(x, ctx_1024, mask_BxS2_bk0, g_xattn, g_ffn, L0_xattn_ln_x_g, L0_xattn_ln_x_b, L0_xattn_ln_l_g, L0_xattn_ln_l_b, L0_xattn_q_gamma, L0_xattn_k_gamma, L0_xattn_W_q, L0_xattn_W_kv, L0_xattn_W_out, L0_xattn_b_out, L0_ffn_norm_g, L0_ffn_norm_b, L0_ffn_slot_g, L0_ffn_slot_b, L0_ffn_scale, L0_ffn_slot_embeds, L0_ffn_Wg, L0_ffn_bg, L0_ffn_Wu, L0_ffn_bu, L0_ffn_Wd, L0_ffn_bd, L1_xattn_gamma_media, L1_xattn_beta_media, L1_xattn_gamma_lat, L1_xattn_beta_lat, L1_xattn_Wq, L1_xattn_bq, L1_xattn_Wkv, L1_xattn_bkv, L1_xattn_Wo, L1_xattn_bo, L1_ffn_router_w, L1_ffn_w_gate, L1_ffn_w_up, L1_ffn_w_down):
    import jax
    import jax.numpy as jnp

    def _L0_xattn_ref(x, latents, mask, ln_x_g, ln_x_b, ln_l_g, ln_l_b, q_gamma, k_gamma, W_q, W_kv, W_out, b_out):
        import jax, jax.numpy as jnp
        import numpy as np
        DIM = 128
        DIM_LATENT = 128
        DIM_HEAD = 64
        INNER = max(DIM, DIM_LATENT)
        HEADS = INNER // DIM_HEAD
        SCALE = DIM_HEAD ** (-0.5)
        LN_EPS = 1e-05
        RMS_EPS = 1e-08

        def layernorm(x, g, b):
            mu = jnp.mean(x, axis=-1, keepdims=True)
            var = jnp.mean(jnp.square(x - mu), axis=-1, keepdims=True)
            return (x - mu) * jax.lax.rsqrt(var + LN_EPS) * g + b

        def rmsnorm(x, gamma):
            n = jnp.linalg.norm(x, axis=-1, keepdims=True) * x.shape[-1] ** (-0.5)
            return x / jnp.maximum(n, RMS_EPS) * gamma
        b, n, _ = x.shape
        nl = latents.shape[1]
        xn = layernorm(x, ln_x_g, ln_x_b)
        ln = layernorm(latents, ln_l_g, ln_l_b)
        q = ln @ W_q
        kv = jnp.concatenate([xn @ W_kv, ln @ W_kv], axis=1)
        k, v = (kv[..., :INNER], kv[..., INNER:])
        to_heads = lambda t: t.reshape(t.shape[0], t.shape[1], HEADS, DIM_HEAD).transpose(0, 2, 1, 3)
        q, k, v = (to_heads(q), to_heads(k), to_heads(v))
        qn = rmsnorm(q, q_gamma) * SCALE
        kn = rmsnorm(k, k_gamma)
        sim = jnp.einsum('bhid,bhjd->bhij', qn, kn)
        full_mask = jnp.pad(mask, ((0, 0), (0, nl)), constant_values=True)
        neg = -jnp.finfo(sim.dtype).max
        sim = jnp.where(full_mask[:, None, None, :], sim, neg)
        attn = jax.nn.softmax(sim.astype(jnp.float32), axis=-1).astype(sim.dtype)
        out = jnp.einsum('bhij,bhjd->bhid', attn, v)
        out = out.transpose(0, 2, 1, 3).reshape(b, nl, INNER)
        return out @ W_out + b_out

    def _L0_ffn_ref(x, norm_g, norm_b, slot_g, slot_b, scale, slot_embeds, Wg, bg, Wu, bu, Wd, bd):
        import jax, jax.numpy as jnp
        import numpy as np
        B, N, D = (4, 512, 128)
        E, S, F = (16, 64, 256)
        DO = 128
        EPS = 1e-05

        def _layernorm(x, g, b):
            mu = jnp.mean(x, axis=-1, keepdims=True)
            var = jnp.mean(jnp.square(x - mu), axis=-1, keepdims=True)
            return (x - mu) * jax.lax.rsqrt(var + EPS) * g + b
        x = _layernorm(x, norm_g, norm_b)
        se = _layernorm(slot_embeds, slot_g, slot_b) * scale
        logits = jnp.einsum('bnd,esd->bnes', x, se)
        dispatch = jax.nn.softmax(logits, axis=1)
        combine = jax.nn.softmax(logits.reshape(x.shape[0], x.shape[1], -1), axis=-1)
        slots = jnp.einsum('bnd,bnes->besd', x, dispatch)
        gate = jax.nn.gelu(jnp.einsum('besd,edf->besf', slots, Wg) + bg[None, :, None, :], approximate=False)
        up = jnp.einsum('besd,edf->besf', slots, Wu) + bu[None, :, None, :]
        eout = jnp.einsum('besf,efo->beso', gate * up, Wd) + bd[None, :, None, :]
        eout = eout.reshape(eout.shape[0], -1, eout.shape[-1])
        return jnp.einsum('bns,bso->bno', combine, eout)

    def _L1_xattn_ref(x, latents, gamma_media, beta_media, gamma_lat, beta_lat, Wq, bq, Wkv, bkv, Wo, bo):
        import jax, jax.numpy as jnp
        import numpy as np
        B, M, N, DIM, DH, H = (8, 512, 64, 128, 128, 8)
        INNER = DH * H
        EPS = 1e-05

        def _layernorm(x, g, b):
            mu = jnp.mean(x, axis=-1, keepdims=True)
            var = jnp.var(x, axis=-1, keepdims=True)
            return (x - mu) * jax.lax.rsqrt(var + EPS) * g + b
        b = x.shape[0]
        xn = _layernorm(x, gamma_media, beta_media)
        ln = _layernorm(latents, gamma_lat, beta_lat)
        q = ln @ Wq + bq
        kv_input = jnp.concatenate([xn, ln], axis=1)
        kv = kv_input @ Wkv + bkv
        k, v = jnp.split(kv, 2, axis=-1)

        def to_heads(t):
            return t.reshape(b, t.shape[1], H, DH).transpose(0, 2, 1, 3)
        q, k, v = (to_heads(q), to_heads(k), to_heads(v))
        q = q * DH ** (-0.5)
        sim = jnp.einsum('bhid,bhjd->bhij', q, k)
        attn = jax.nn.softmax(sim, axis=-1)
        out = jnp.einsum('bhij,bhjd->bhid', attn, v)
        out = out.transpose(0, 2, 1, 3).reshape(b, -1, INNER)
        return out @ Wo + bo

    def _L1_ffn_ref(x, router_w, w_gate, w_up, w_down):
        import jax, jax.numpy as jnp
        import numpy as np
        from jax import lax
        DIM = 128
        HID = 256
        E = 8
        K = 2
        B, T = (2, 64)
        Bb, Tt, D = x.shape
        N = Bb * Tt
        xf = x.reshape(N, D)
        logits = xf @ router_w.T
        routing = jax.nn.softmax(logits, axis=-1)
        top_w, top_i = lax.top_k(routing, K)
        top_w = top_w / jnp.sum(top_w, axis=-1, keepdims=True)
        combine = jnp.zeros((N, E), dtype=x.dtype)
        combine = combine.at[jnp.arange(N)[:, None], top_i].add(top_w)
        g = jnp.einsum('nd,ehd->neh', xf, w_gate)
        u = jnp.einsum('nd,ehd->neh', xf, w_up)
        h = jax.nn.silu(g) * u
        y = jnp.einsum('neh,edh->ned', h, w_down)
        out = jnp.einsum('ned,ne->nd', y, combine)
        return out.reshape(Bb, Tt, D)
    x = x + jnp.tanh(g_xattn[0]) * _L0_xattn_ref(ctx_1024, _layernorm(x, axis=-1), mask_BxS2_bk0, L0_xattn_ln_x_g, L0_xattn_ln_x_b, L0_xattn_ln_l_g, L0_xattn_ln_l_b, L0_xattn_q_gamma, L0_xattn_k_gamma, L0_xattn_W_q, L0_xattn_W_kv, L0_xattn_W_out, L0_xattn_b_out)
    x = x + jnp.tanh(g_ffn[0]) * _L0_ffn_ref(_layernorm(x, axis=-1), L0_ffn_norm_g, L0_ffn_norm_b, L0_ffn_slot_g, L0_ffn_slot_b, L0_ffn_scale, L0_ffn_slot_embeds, L0_ffn_Wg, L0_ffn_bg, L0_ffn_Wu, L0_ffn_bu, L0_ffn_Wd, L0_ffn_bd)
    x = x + jnp.tanh(g_xattn[1]) * _L1_xattn_ref(ctx_1024, _layernorm(x, axis=-1), L1_xattn_gamma_media, L1_xattn_beta_media, L1_xattn_gamma_lat, L1_xattn_beta_lat, L1_xattn_Wq, L1_xattn_bq, L1_xattn_Wkv, L1_xattn_bkv, L1_xattn_Wo, L1_xattn_bo)
    x = x + jnp.tanh(g_ffn[1]) * _L1_ffn_ref(_layernorm(x, axis=-1), L1_ffn_router_w, L1_ffn_w_gate, L1_ffn_w_up, L1_ffn_w_down)
    return x

_drawn_inputs = setup_inputs


def setup_inputs(seed=0):
    import zlib

    import numpy as np

    out = dict(_drawn_inputs(seed))
    spreads = {'g_ffn': (-1.0, 0.585),
     'L0_xattn_ln_x_g': (1.0, 0.2),
     'L0_xattn_ln_x_b': (0.0, 0.1),
     'L0_xattn_ln_l_g': (1.0, 0.2),
     'L0_xattn_ln_l_b': (0.0, 0.1),
     'L0_xattn_q_gamma': (1.0, 0.2),
     'L0_xattn_k_gamma': (1.0, 0.2),
     'L0_xattn_b_out': (0.0, 0.1),
     'L0_ffn_norm_g': (1.0, 0.2),
     'L0_ffn_norm_b': (0.0, 0.1),
     'L0_ffn_slot_g': (1.0, 0.2),
     'L0_ffn_slot_b': (0.0, 0.1),
     'L0_ffn_bg': (0.0, 0.1),
     'L0_ffn_bu': (0.0, 0.1),
     'L0_ffn_bd': (0.0, 0.1),
     'L1_xattn_gamma_media': (1.0, 0.6),
     'L1_xattn_beta_media': (0.0, 0.457),
     'L1_xattn_gamma_lat': (1.0, 0.6),
     'L1_xattn_beta_lat': (0.0, 0.391),
     'L1_xattn_bq': (0.0, 2.0),
     'L1_xattn_bkv': (0.0, 0.1),
     'L1_xattn_bo': (0.0, 0.1)}
    factors = {'L1_xattn_Wq': 7.408}
    for name, (base, spread) in spreads.items():
        noise = np.random.default_rng([zlib.crc32(name.encode()), seed]).standard_normal(out[name].shape)
        drawn = base * np.exp(spread * noise) if base else spread * noise
        out[name] = jnp.asarray(drawn.astype(out[name].dtype))
    for name, factor in factors.items():
        out[name] = (out[name] * factor).astype(out[name].dtype)
    return out
```

```python
from contextlib import ExitStack

import concourse.bass as bass
from concourse import mybir

F32 = mybir.dt.float32
F32R = mybir.dt.float32r
U8 = mybir.dt.uint8
U32 = mybir.dt.uint32
ALU = mybir.AluOpType
ACT = mybir.ActivationFunctionType
AX = mybir.AxisListType

P = 128
BATCHES = 64
SEQ = 64
D = 128
PAIRS = BATCHES // 2
OB = 8
OP = OB // 2
OT = OB * SEQ
OCTETS = BATCHES // OB
EPS = 1e-5
RMS_EPS = 1e-8
MASKED = -1e30


def need(eng, sem, count):
    if isinstance(count, int) and count <= 0:
        return
    eng.wait_ge(sem, count)


def walk(eng, body):
    body(-1, 1)
    body(0, 0)
    if OCTETS > 2:
        with eng.Fori(0, (OCTETS - 2) // 2) as turn:
            body(turn * 2 + 1, 1)
            body(turn * 2 + 2, 0)
    body(OCTETS - 1, 1)


def has_core(o):
    return not (isinstance(o, int) and o < 0)


def has_head(o):
    return not (isinstance(o, int) and o >= OCTETS - 1)


def column(vector):
    return vector.rearrange("(d a) -> d a", a=1)


def all_rows(vector):
    return vector.partition_broadcast(P)


def over(ap, n, at):
    ap = ap.unsqueeze(at)
    shape = list(ap.shape)
    shape[at] = n
    return ap.to_broadcast(shape)


class Chip:

    def __init__(self, nc, ins, out, keep):
        self.nc, self.ins, self.out, self.keep = nc, ins, out, keep
        sb = self.sb(keep)
        self.x = sb("x", [P, PAIRS, D])
        self.bn = sb("x_bn", [P, PAIRS, 6])
        self.stats = sb("x_stats", [P, PAIRS, 2])
        self.inv = sb("x_inv", [P, PAIRS])
        self.cstats = sb("ctx_stats", [P, PAIRS, 2])
        self.cinv = sb("ctx_inv", [P, PAIRS])
        self.ident = sb("ident", [P, P])
        self.gates = sb("gates", [P, 4])
        self.stored = keep.enter_context(nc.semaphore("out_stored"))

    def sb(self, ctx):
        def make(name, shape, dt=F32):
            return ctx.enter_context(self.nc.sbuf_tensor(name, shape, dt))
        return make

    def bank(self, ctx, name, shape=None, banks=1):
        shape = shape or [P, 512 * banks]
        return ctx.enter_context(self.nc.psum_tensor(name, shape, F32))

    def sem(self, ctx):
        sems = []

        def clear():
            self.nc.clear_and_free_semaphores(sems)
            self.nc.all_engine_barrier()

        def make(name):
            sems.append(self.nc.alloc_semaphore(name=name))
            return sems[-1]

        ctx.callback(clear)
        return make


def product3(pe, out, stationary, moving, start=True, stop=True, **more):
    pe.matmul(out, stationary[0], moving[0], start=start, stop=False, **more)
    pe.matmul(out, stationary[0], moving[1], start=False, stop=False, **more)
    return pe.matmul(out, stationary[1], moving[0], start=False, stop=stop, **more)


def tokens(ap):
    return ap.rearrange("(p b) n d -> (b n) p d", b=2)


def stage_start(c):
    nc, ins = c.nc, c.ins
    with ExitStack() as ctx:
        sb, sem = c.sb(ctx), c.sem(ctx)
        graw = sb("gates_raw", [P, 4])
        loaded, gate_loaded = [sem(f"x_loaded{n}") for n in range(4)], sem("gates_loaded")
        zeroed = sem("ident_zeroed")
        block = ctx.enter_context(nc.Block())

        @block.sync
        def _(sp):
            for q in range(4):
                s = slice(q * PAIRS // 4, (q + 1) * PAIRS // 4)
                sp.dma_start(c.x[:, s, :], tokens(ins["x"])[:, s, :]).then_inc(loaded[q], 16)
            for g in range(4):
                src = ins["g_ffn" if g % 2 else "g_xattn"][g // 2:g // 2 + 1]
                sp.dma_start(graw[:, g:g + 1], src.partition_broadcast(P)).then_inc(gate_loaded, 16)

        @block.gpsimd
        def _(pool):
            pool.memset(c.ident[:], 0.0).then_inc(zeroed, 1)
            pool.wait_ge(zeroed, 1)
            pool.affine_select(out=c.ident[:], in_=c.ident[:], compare_op=ALU.not_equal, fill=1.0, base=0,
                               pattern=[[-1, P]], channel_multiplier=1)

        @block.scalar
        def _(act):
            act.wait_ge(gate_loaded, 64)
            act.activation(c.gates[:], graw[:], ACT.Tanh)

        @block.vector
        def _(dve):
            for t in range(PAIRS):
                if t % (PAIRS // 4) == 0:
                    dve.wait_ge(loaded[t // (PAIRS // 4)], 16)
                dve.bn_stats(c.bn[:, t, :], c.x[:, t, :])


def stage_attention0(c):
    nc, ins = c.nc, c.ins
    HEADS, DH = 2, 64
    with ExitStack() as ctx:
        sb, sem = c.sb(ctx), c.sem(ctx)
        ctx_sb = sb("ctx0", [P, PAIRS, D])
        cstats, cinv = c.cstats, c.cinv
        cbn = sb("ctx_bn0", [P, PAIRS, 6])
        work = sb("inv_work0", [P, 2, PAIRS])
        w_q, w_kv, w_out = sb("w_q0", [P, D]), sb("w_kv0", [P, 2 * D]), sb("w_out0", [P, D])
        cols = sb("norm_cols0", [P, 4])
        gam = sb("qk_gamma0", [P, 2])
        gam_raw = sb("q_gamma_raw0", [P, 1])
        bout = sb("b_out0", [P, D])
        gbout = sb("gated_b_out0", [P, D])
        mask_raw = sb("mask_raw", [1, BATCHES * SEQ], U8)
        bias = sb("mask_bias", [1, BATCHES * SEQ])
        ones = sb("ones_row0", [1, P])
        xh, ch = sb("x_hat0", [P, OP, D]), sb("ctx_hat0", [P, OP, D])
        kvin = sb("kv_in0", [P, OB, P])
        lat = sb("latents0", [P, OP, P])
        kv = [sb(f"kv0_{i}", [P, OB, 2 * D]) for i in range(2)]
        q = sb("q0", [P, OP, D])
        sq_k, sq_q = sb("sq_k", [P, OB, D]), sb("sq_q", [P, OP, D])
        ss = sb("sum_sq", [P, 24])
        root = sb("rms", [P, 24])
        kn, qn = sb("kn", [P, OB, D]), sb("qn", [P, OP, D])
        kT = [sb(f"kT{i}", [P, OB, P]) for i in range(2)]
        qT = [sb(f"qT{i}", [P, OB, P]) for i in range(2)]
        pr = sb("probs0", [P, OB, P])
        nmax, rs = sb("neg_max0", [P, OB]), sb("row_sum0", [P, OB])
        pT = sb("probsT0", [P, OB, P])
        oT = sb("oT0", [P, OB, SEQ])
        fresh = sb("x_fresh0", [P, OP, D])
        bn = sb("bn_a", [P, OP, 6])

        X, K = c.bank(ctx, "psX", [P, OB, P], 2), c.bank(ctx, "psK", [P, OB // 2, 2 * D], 2)
        S, T = c.bank(ctx, "psS", [P, OB, P], 2), c.bank(ctx, "psT", [P, OB, P], 2)

        names = ("wq_loaded cols_loaded mask_loaded ctx_bn ctx_aggr inv_a inv_b inv_done bias_a "
                 "mask_ready gam_ready gbout_ready zeroed ones_ready x_hat ctx_hat tx kv_in kv_proj kv_copied q_proj "
                 "q_copied squared sum_sq root root_max root_inv kn qn kt qt kT_ready qT_ready sim neg_max shifted "
                 "exped row_sum row_inv probs_normed pt probsT av oT_ready out_proj x_biased x_new bn aggr")
        s = {n: sem("a_" + n) for n in names.split()}
        ctx_loaded = [sem(f"a_ctx_loaded{n}") for n in range(4)]
        block = ctx.enter_context(nc.Block())

        def half_of(g):
            return slice(g * OB // 2, (g + 1) * OB // 2)

        @block.sync
        def _(sp):
            for n in range(4):
                r = slice(n * PAIRS // 4, (n + 1) * PAIRS // 4)
                sp.dma_start(ctx_sb[:, r, :], tokens(ins["ctx_1024"])[:, r, :]).then_inc(ctx_loaded[n], 16)
            for n, name in enumerate(("ln_x_g", "ln_x_b", "ln_l_g", "ln_l_b")):
                sp.dma_start(cols[:, n:n + 1], column(ins["L0_xattn_" + name])).then_inc(s["cols_loaded"], 16)
            for h in range(HEADS):
                r = slice(h * DH, (h + 1) * DH)
                sp.dma_start(gam_raw[r, :], column(ins["L0_xattn_q_gamma"])).then_inc(s["cols_loaded"], 16)
                sp.dma_start(gam[r, 1:2], column(ins["L0_xattn_k_gamma"])).then_inc(s["cols_loaded"], 16)
            sp.dma_start(bout[:], all_rows(ins["L0_xattn_b_out"])).then_inc(s["cols_loaded"], 16)
            sp.dma_start(w_q[:], ins["L0_xattn_W_q"]).then_inc(s["wq_loaded"], 16)
            sp.dma_start(w_kv[:], ins["L0_xattn_W_kv"]).then_inc(s["wq_loaded"], 16)
            sp.dma_start(w_out[:], ins["L0_xattn_W_out"]).then_inc(s["wq_loaded"], 16)
            sp.dma_start(mask_raw[:], ins["mask_BxS2_bk0"].rearrange("(a b) k -> a (b k)", a=1)
                         ).then_inc(s["mask_loaded"], 16)

        @block.gpsimd
        def _(pool):
            pool.memset(ones[:], 1.0).then_inc(s["ones_ready"], 1)
            for i in range(2):
                pool.memset(qT[i][:], 0.0).then_inc(s["zeroed"], 1)
            pool.wait_ge(s["cols_loaded"], 16 * 9)
            pool.tensor_scalar(gam[:, 0:1], gam_raw[:], float(DH) ** -0.5, None, ALU.mult).then_inc(s["gam_ready"], 1)
            pool.tensor_scalar(gbout[:], bout[:], c.gates[:, 0:1], None, ALU.mult).then_inc(s["gbout_ready"], 1)
            pool.wait_ge(s["mask_loaded"], 16)
            pool.tensor_copy(bias[:], mask_raw[:]).then_inc(s["bias_a"], 1)
            pool.wait_ge(s["bias_a"], 1)
            pool.tensor_scalar(bias[:], bias[:], -MASKED, MASKED, ALU.mult, ALU.add).then_inc(s["mask_ready"], 1)
            pool.wait_ge(s["gbout_ready"], 1)

            def body(o, par):
                if has_core(o):
                    for g in range(2):
                        need(pool, s["row_inv"], 2 * o + g + 1)
                        r = half_of(g)
                        pool.tensor_tensor(pr[:, r, :], pr[:, r, :], over(rs[:, r], P, 2), ALU.mult
                                           ).then_inc(s["probs_normed"], 1)
                if has_core(o):
                    need(pool, s["x_hat"], o + 1)
                    xo = c.x[:, bass.ds(4 * o, OP), :]
                    pool.tensor_tensor(xo, xo, over(gbout[:], OP, 1), ALU.add).then_inc(s["x_biased"], 1)

            walk(pool, body)

        @block.vector
        def _(dve):
            for t in range(PAIRS):
                if t % (PAIRS // 4) == 0:
                    dve.wait_ge(ctx_loaded[t // (PAIRS // 4)], 16)
                dve.bn_stats(cbn[:, t, :], ctx_sb[:, t, :]).then_inc(s["ctx_bn"], 1)
            for t in range(PAIRS):
                dve.wait_ge(s["ctx_bn"], t + 1)
                dve.bn_aggr(cstats[:, t, :], cbn[:, t, :]).then_inc(s["ctx_aggr"], 1)
            dve.wait_ge(s["ctx_aggr"], PAIRS)
            x_stats(c, dve, s["aggr"])
            norm_scales(dve, work, [(c.stats, True), (cstats, False)], s["inv_a"])
            dve.wait_ge(s["inv_b"], 2)
            dve.reciprocal(c.inv[:], work[:, 0, :]).then_inc(s["inv_done"], 1)
            dve.reciprocal(cinv[:], work[:, 1, :]).then_inc(s["inv_done"], 1)
            dve.wait_ge(s["inv_done"], 2)

            def finish(o):
                need(dve, s["out_proj"], o + 1)
                need(dve, s["x_biased"], o + 1)
                xo = c.x[:, bass.ds(4 * o, OP), :]
                dve.scalar_tensor_tensor(fresh[:], T[:, 0:OP, :], c.gates[:, 0:1], xo, ALU.mult, ALU.add
                                         ).then_inc(s["x_new"], 1)
                keep_fresh(c, dve, o, fresh, bn, s["x_new"], s["bn"])

            def body(o, par):
                h = o + 1
                if has_head(o):
                    need(dve, s["tx"], h)
                    for p in range(OP):
                        t = 4 * h + p
                        last = dve.tensor_scalar(xh[:, p, :], c.x[:, t, :], c.stats[:, t, 0:1], c.inv[:, bass.ds(t, 1)],
                                                 ALU.subtract, ALU.mult)
                    last.then_inc(s["x_hat"], 1)
                    for p in range(OP):
                        t = 4 * h + p
                        last = dve.tensor_scalar(ch[:, p, :], ctx_sb[:, t, :], cstats[:, t, 0:1], cinv[:, bass.ds(t, 1)],
                                                 ALU.subtract, ALU.mult)
                    last.then_inc(s["ctx_hat"], 1)
                if not isinstance(o, int) or o > 0:
                    finish(o - 1)
                if has_core(o):
                    need(dve, s["pt"], o)
                    for g in range(2):
                        r = half_of(g)
                        need(dve, s["sim"], 2 * o + g + 1)
                        dve.tensor_reduce(nmax[:, r], S[:, r, :], AX.X, ALU.max, negate=True).then_inc(s["neg_max"], 1)
                        need(dve, s["neg_max"], 2 * o + g + 1)
                        dve.tensor_tensor(pr[:, r, :], S[:, r, :], over(nmax[:, r], P, 2), ALU.add
                                          ).then_inc(s["shifted"], 1)
                    for g in range(2):
                        r = half_of(g)
                        need(dve, s["exped"], 2 * o + g + 1)
                        dve.tensor_reduce(rs[:, r], pr[:, r, :], AX.X, ALU.add).then_inc(s["row_sum"], 1)
                        need(dve, s["row_sum"], 2 * o + g + 1)
                        dve.reciprocal(rs[:, r], rs[:, r]).then_inc(s["row_inv"], 1)
                if has_head(o):
                    k = kv[1 - par][:, :, 0:D]
                    parts = [(k[:, half_of(0), :], sq_k[:, half_of(0), :], slice(0, 8)), (q[:], sq_q[:], slice(16, 24)),
                             (k[:, half_of(1), :], sq_k[:, half_of(1), :], slice(8, 16))]
                    for n, (src, square, r) in enumerate(parts):
                        if n == 1:
                            need(dve, s["q_copied"], h + 1)
                        else:
                            need(dve, s["kv_copied"], 2 * h + 1 + n // 2)
                        need(dve, s["sum_sq"], 3 * h)
                        dve.tensor_tensor(square, src, src, ALU.mult).then_inc(s["squared"], 1)
                        need(dve, s["squared"], 3 * h + n + 1)
                        dve.tensor_reduce(ss[:, r], square.rearrange("p b (h d) -> p b h d", h=HEADS), AX.X, ALU.add
                                          ).then_inc(s["sum_sq"], 1)
                    need(dve, s["root"], h + 1)
                    dve.tensor_scalar(root[:], root[:], RMS_EPS, None, ALU.max).then_inc(s["root_max"], 1)
                    need(dve, s["root_max"], h + 1)
                    dve.reciprocal(root[:], root[:]).then_inc(s["root_inv"], 1)
                    need(dve, s["root_inv"], h + 1)
                    need(dve, s["kt"], h)
                    need(dve, s["qt"], h)
                    dve.tensor_tensor(kn[:].rearrange("p b (h d) -> p b h d", h=HEADS),
                                      kv[1 - par][:, :, 0:D].rearrange("p b (h d) -> p b h d", h=HEADS),
                                      over(root[:, 0:16].rearrange("p (b h) -> p b h", h=HEADS), DH, 3), ALU.mult
                                      ).then_inc(s["kn"], 1)
                    dve.tensor_tensor(qn[:].rearrange("p b (h d) -> p (b h) d", h=HEADS),
                                      q[:].rearrange("p b (h d) -> p (b h) d", h=HEADS),
                                      over(root[:, 16:24], DH, 2), ALU.mult).then_inc(s["qn"], 1)

            walk(dve, body)
            finish(OCTETS - 1)

        @block.scalar
        def _(act):
            for n in range(2):
                act.wait_ge(s["inv_a"], n + 1)
                act.activation(work[:, n, :], work[:, n, :], ACT.Sqrt).then_inc(s["inv_b"], 1)
            act.wait_ge(s["cols_loaded"], 16 * 9)
            act.wait_ge(s["gam_ready"], 1)
            act.wait_ge(s["zeroed"], 2)

            def body(o, par):
                h = o + 1
                if has_head(o):
                    need(act, s["tx"], h + 1)
                    need(act, s["q_proj"], h)
                    need(act, s["kv_proj"], 2 * h)
                    act.activation(kvin[:, :, SEQ:P], X[:, OP:OB, :].rearrange("p t (b n) -> p (t b) n", b=2),
                                   ACT.Identity, bias=cols[:, 3:4], scale=cols[:, 2:3]).then_inc(s["kv_in"], 1)
                    act.activation(lat[:], X[:, OP:OB, :], ACT.Identity, bias=cols[:, 3:4], scale=cols[:, 2:3]
                                   ).then_inc(s["kv_in"], 1)
                    act.activation(kvin[:, :, 0:SEQ], X[:, 0:OP, :].rearrange("p t (b n) -> p (t b) n", b=2),
                                   ACT.Identity, bias=cols[:, 1:2], scale=cols[:, 0:1]).then_inc(s["kv_in"], 1)
                if has_core(o):
                    for g in range(2):
                        r = half_of(g)
                        need(act, s["shifted"], 2 * o + g + 1)
                        act.activation(pr[:, r, :], pr[:, r, :], ACT.Exp).then_inc(s["exped"], 1)
                if has_head(o):
                    need(act, s["kv_proj"], 2 * h + 1)
                    need(act, s["squared"], 3 * (h - 1))
                    need(act, s["kn"], h - 1)
                    need(act, s["av"], h - 1)
                    act.copy(kv[1 - par][:, 0:OB // 2, :], K[:]).then_inc(s["kv_copied"], 1)
                    need(act, s["q_proj"], h + 1)
                    need(act, s["qn"], h)
                    need(act, s["squared"], 3 * h)
                    act.copy(q[:], X[:, 0:OP, :]).then_inc(s["q_copied"], 1)
                if has_head(o):
                    need(act, s["kv_proj"], 2 * h + 2)
                    act.copy(kv[1 - par][:, OB // 2:OB, :], K[:]).then_inc(s["kv_copied"], 1)
                if has_core(o):
                    need(act, s["pt"], o + 1)
                    need(act, s["av"], o)
                    for g in range(2):
                        act.copy(pT[:, half_of(g), :], T[:, half_of(g), :]).then_inc(s["probsT"], 1)
                if has_head(o):
                    need(act, s["sum_sq"], 3 * h + 3)
                    need(act, s["kn"], h)
                    need(act, s["qn"], h)
                    act.activation(root[:], ss[:], ACT.Sqrt, scale=1.0 / DH).then_inc(s["root"], 1)
                if has_core(o):
                    need(act, s["av"], o + 1)
                    need(act, s["out_proj"], o)
                    act.copy(oT[0:DH, :, :], S[0:DH, :, 0:SEQ])
                    act.copy(oT[DH:P, :, :], S[DH:P, :, SEQ:P]).then_inc(s["oT_ready"], 1)
                if has_head(o):
                    need(act, s["kt"], h + 1)
                    need(act, s["sim"], 2 * (h - 1))
                    act.activation(kT[1 - par][:], X[:], ACT.Identity, scale=gam[:, 1:2]).then_inc(s["kT_ready"], 1)
                    need(act, s["qt"], h + 1)
                    for hd in range(HEADS):
                        r = slice(hd * DH, (hd + 1) * DH)
                        last = act.activation(
                            qT[1 - par][r, :, hd * SEQ:(hd + 1) * SEQ],
                            K[r, 0:2, :].rearrange("p a (t n) -> p (a t) n", n=SEQ),
                            ACT.Identity, scale=gam[r, 0:1])
                    last.then_inc(s["qT_ready"], 1)

            walk(act, body)

        @block.tensor
        def _(pe):
            pe.wait_ge(s["wq_loaded"], 48)

            def body(o, par):
                h = o + 1
                if has_head(o):
                    need(pe, s["x_hat"], h + 1)
                    need(pe, s["ctx_hat"], h + 1)
                    need(pe, s["kT_ready"], h)
                    for p in range(OP):
                        pe.transpose(X[:, p, :], ch[:, p, :], c.ident[:])
                    for p in range(OP):
                        last = pe.transpose(X[:, OP + p, :], xh[:, p, :], c.ident[:])
                    last.then_inc(s["tx"], 1)
                if has_core(o):
                    need(pe, s["kT_ready"], o + 1)
                    need(pe, s["qT_ready"], o + 1)
                    if isinstance(o, int) and o == 0:
                        pe.wait_ge(s["ones_ready"], 1)
                        pe.wait_ge(s["mask_ready"], 1)
                    need(pe, s["oT_ready"], o)
                    for b in range(OB):
                        pe.matmul(S[:, b, :], qT[par][:, b, :], kT[par][:, b, :], start=True, stop=False)
                        last = pe.matmul(S[:, b, 0:SEQ], ones[:], bias[0:1, bass.ds((8 * o + b) * SEQ, SEQ)],
                                         start=False, stop=True)
                        if b % (OB // 2) == OB // 2 - 1:
                            last.then_inc(s["sim"], 1)
                if has_head(o):
                    need(pe, s["kv_in"], 3 * h + 3)
                    need(pe, s["qT_ready"], h)
                    for b in range(OB // 2):
                        last = pe.matmul(K[:, b, :], kvin[:, b, :], w_kv[:], start=True, stop=True)
                    last.then_inc(s["kv_proj"], 1)
                    for p in range(OP):
                        last = pe.matmul(X[:, p, :], lat[:, p, :], w_q[:], start=True, stop=True)
                    last.then_inc(s["q_proj"], 1)
                if has_head(o):
                    need(pe, s["kv_copied"], 2 * h + 1)
                    for b in range(OB // 2):
                        last = pe.matmul(K[:, b, :], kvin[:, OB // 2 + b, :], w_kv[:], start=True, stop=True)
                    last.then_inc(s["kv_proj"], 1)
                if has_core(o):
                    need(pe, s["probs_normed"], 2 * o + 2)
                    need(pe, s["x_new"], o)
                    for b in range(OB):
                        last = pe.transpose(T[:, b, :], pr[:, b, :], c.ident[:])
                    last.then_inc(s["pt"], 1)
                if has_core(o):
                    need(pe, s["shifted"], 2 * o + 2)
                    for b in range(OB):
                        if b % (OB // 2) == 0:
                            need(pe, s["probsT"], 2 * o + 1 + b // (OB // 2))
                        last = pe.matmul(S[:, b, :], kv[par][:, b, D:2 * D], pT[:, b, :], start=True, stop=True)
                    last.then_inc(s["av"], 1)
                    need(pe, s["oT_ready"], o + 1)
                    for p in range(OP):
                        last = pe.matmul(T[:, p, :], oT[:, 2 * p:2 * p + 2, :], w_out[:], start=True, stop=True)
                    last.then_inc(s["out_proj"], 1)
                if has_head(o):
                    need(pe, s["kn"], h + 1)
                    need(pe, s["q_copied"], h + 1)
                    for b in range(OB):
                        last = pe.transpose(X[:, b, :], kn[:, b, :], c.ident[:])
                    last.then_inc(s["kt"], 1)
                    need(pe, s["qn"], h + 1)
                    need(pe, s["kv_copied"], 2 * h + 2)
                    for p in range(OP):
                        last = pe.transpose(K[:, p // 2, (p % 2) * D:(p % 2 + 1) * D], qn[:, p, :], c.ident[:])
                    last.then_inc(s["qt"], 1)

            walk(pe, body)


def stage_experts0(c):
    nc, ins = c.nc, c.ins
    E, F = 16, 2 * P
    CH = E // 2
    EH = 2 * E
    LAST = CH * OCTETS - 1
    with ExitStack() as ctx:
        sb, sem = c.sb(ctx), c.sem(ctx)
        wg = [sb(f"w_gate_{n}", [P, E, F], F32R) for n in ("hi", "lo")]
        wu = [sb(f"w_up_{n}", [P, E, F], F32R) for n in ("hi", "lo")]
        wd = sb("w_down", [P, E, 2, D])
        seT = [sb(f"slotsT_{n}", [P, E * SEQ], F32R) for n in ("hi", "lo")]
        bd = sb("b_down", [P, E, D])
        bcol = sb("b_cols", [P, 2, EH])
        ng, nb = sb("norm_g", [P, D]), sb("norm_b", [P, D])
        slot_cols = sb("slot_cols", [P, 3])
        slot_gb = sb("slot_gb", [P, 2])
        sst, sinv = sb("slot_stats", [P, CH, 2]), sb("slot_inv", [P, CH])
        xh = sb("x_hat1", [P, OP, D])
        xn = [sb(f"x_normed1_{i}", [P, OP, D]) for i in range(2)]
        lnT = [[sb(f"x_normedT_{n}{i}", [P, OT], F32R) for n in ("hi", "lo")] for i in range(2)]
        ca = [sb(f"combine{i}", [P, OP, E * SEQ]) for i in range(2)]
        na, ra = sb("neg_max_c", [P, OP]), [sb(f"combine_inv{i}", [P, OP]) for i in range(2)]
        eb = [sb(f"dispatchT{i}", [P, OB, SEQ]) for i in range(2)]
        nm, rb = sb("neg_max_d", [P, OB]), sb("dispatch_inv", [P, OB])
        dn = sb("dispatch", [P, OP, P])
        ct = [[sb(f"combineT{i}{e}", [P, OP, P]) for e in range(2)] for i in range(2)]
        sl = [[sb(f"slots_{n}{i}", [P, 2, OB, SEQ], F32R) for n in ("hi", "lo")] for i in range(2)]
        gel = [sb(f"gelu{i}", [P, OT]) for i in range(2)]
        hid = [sb(f"hidden{i}", [P, 2, OT]) for i in range(2)]
        eo = [sb(f"expert_out{i}", [P, OP, D]) for i in range(2)]
        fresh, bn = xh, sb("bn_b", [P, OP, 6])

        G = [c.bank(ctx, f"psG{i}") for i in range(2)]
        U = [c.bank(ctx, f"psU{i}") for i in range(2)]
        OUT, DN = c.bank(ctx, "psOut", [P, OP, D]), c.bank(ctx, "psDown", [P, OP, D])
        M = c.bank(ctx, "psM", [P, 2, 512], 2)
        M0 = M[:, 0, :]
        M1 = M[:, 1, :].rearrange("p (t s) -> p t s", t=OP)

        names = ("wg_loaded wu_loaded wd_loaded slots_loaded vecs_loaded rows_loaded split_hi split_lo zeroed "
                 "aggr inv_a inv_b inv_done slot_bn slot_aggr slot_gb slot_hat slot_tx slot_T slot_hi slot_lo b_t b_ready "
                 "x_hat x_scaled x_normed tx lnT_hi lnT_lo la la_max la_exp la_inv la_gated lb lb_max lb_shifted lb_exp "
                 "lb_sum lb_inv eb_normed td d_ready ct_t ct_ready sl sl_hi sl_lo gate up gelu hidden down eo_ready "
                 "combined x_new bn")
        s = {n: sem("b_" + n) for n in names.split()}
        block = ctx.enter_context(nc.Block())
        b_rows = eo[0][0:EH, 0:2, :]
        work = gel[0][:, 0:2 * PAIRS].rearrange("p (a t) -> p a t", a=2)
        sbn = gel[1][:, 0:6 * CH].rearrange("p (t n) -> p t n", n=6)
        se_raw = hid[0][:].rearrange("p a (b d) -> p (a b) d", d=D)
        se_hat = hid[1][:].rearrange("p a (b d) -> p (a b) d", d=D)
        se_T = hid[0][:].rearrange("p a n -> p (a n)")
        wg_raw = ca[0][:].rearrange("p t n -> p (t n)").rearrange("p (e f) -> p e f", e=E)
        wu_raw = ca[1][:].rearrange("p t n -> p (t n)").rearrange("p (e f) -> p e f", e=E)

        def exists(o, ch, ahead):
            return not isinstance(o, int) or 0 <= CH * o + ch + ahead <= LAST

        @block.sync
        def _(sp):
            sp.dma_start(se_raw, ins["L0_ffn_slot_embeds"].rearrange("e s d -> (e s) d")
                         .rearrange("(c p) d -> p c d", p=P)).then_inc(s["slots_loaded"], 16)
            for n, name in enumerate(("slot_g", "slot_b")):
                sp.dma_start(slot_cols[:, n:n + 1], column(ins["L0_ffn_" + name])).then_inc(s["vecs_loaded"], 16)
            sp.dma_start(slot_cols[:, 2:3], all_rows(ins["L0_ffn_scale"])).then_inc(s["vecs_loaded"], 16)
            sp.dma_start(ng[:], all_rows(ins["L0_ffn_norm_g"])).then_inc(s["vecs_loaded"], 16)
            sp.dma_start(nb[:], all_rows(ins["L0_ffn_norm_b"])).then_inc(s["vecs_loaded"], 16)
            for n, name in enumerate(("bg", "bu")):
                sp.dma_start(b_rows[:, n, :], ins["L0_ffn_" + name].rearrange("e (h f) -> (e h) f", h=2)
                             ).then_inc(s["rows_loaded"], 16)
            sp.dma_start(wg_raw, ins["L0_ffn_Wg"].rearrange("e d f -> d e f")).then_inc(s["wg_loaded"], 16)
            sp.dma_start(wu_raw, ins["L0_ffn_Wu"].rearrange("e d f -> d e f")).then_inc(s["wu_loaded"], 16)
            sp.dma_start(wd[:], ins["L0_ffn_Wd"].rearrange("e (h f) o -> f e h o", h=2)).then_inc(s["wd_loaded"], 16)
            sp.dma_start(bd[:].rearrange("p e d -> p (e d)"),
                         all_rows(ins["L0_ffn_bd"].rearrange("e d -> (e d)"))).then_inc(s["wd_loaded"], 16)

        @block.gpsimd
        def _(pool):
            pool.wait_ge(s["vecs_loaded"], 16 * 5)
            pool.tensor_scalar(slot_gb[:], slot_cols[:, 0:2], slot_cols[:, 2:3], None, ALU.mult
                               ).then_inc(s["slot_gb"], 1)
            for i in range(2):
                for e in range(2):
                    pool.memset(ct[i][e][:], 0.0).then_inc(s["zeroed"], 1)

            def body(o, par):
                for ch in range(CH):
                    k = o * CH + ch
                    if ch == 0 and has_head(o):
                        need(pool, s["x_hat"], o + 2)
                        need(pool, s["sl"], 8 * o)
                        need(pool, s["tx"], o)
                        t = xn[1 - par]
                        pool.tensor_tensor(t[:], xh[:], over(ng[:], OP, 1), ALU.mult).then_inc(s["x_scaled"], 1)
                        need(pool, s["x_scaled"], o + 2)
                        pool.tensor_tensor(t[:], t[:], over(nb[:], OP, 1), ALU.add).then_inc(s["x_normed"], 1)
                    if exists(o, ch, 2):
                        need(pool, s["lb_inv"], k + 3)
                        e = eb[ch % 2]
                        pool.tensor_tensor(e[:], e[:], over(rb[:], SEQ, 2), ALU.mult).then_inc(s["eb_normed"], 1)

            walk(pool, body)

        @block.vector
        def _(dve):
            x_stats(c, dve, s["aggr"])
            dve.wait_ge(s["slots_loaded"], 16)
            for t in range(CH):
                dve.bn_stats(sbn[:, t, :], se_raw[:, t, :]).then_inc(s["slot_bn"], 1)
            for t in range(CH):
                dve.wait_ge(s["slot_bn"], t + 1)
                dve.bn_aggr(sst[:, t, :], sbn[:, t, :]).then_inc(s["slot_aggr"], 1)
            dve.wait_ge(s["slot_aggr"], CH)
            norm_scales(dve, work, [(c.stats, True), (sst, False)], s["inv_a"])
            dve.wait_ge(s["inv_b"], 2)
            dve.reciprocal(c.inv[:], work[:, 0, 0:PAIRS]).then_inc(s["inv_done"], 1)
            dve.reciprocal(sinv[:], work[:, 1, 0:CH]).then_inc(s["inv_done"], 1)
            dve.wait_ge(s["inv_done"], 2)
            for t in range(CH):
                dve.tensor_scalar(se_hat[:, t, :], se_raw[:, t, :], sst[:, t, 0:1], sinv[:, t:t + 1],
                                  ALU.subtract, ALU.mult).then_inc(s["slot_hat"], 1)
            dve.wait_ge(s["b_t"], 1)
            dve.tensor_copy(bcol[:], DN[:, 0, 0:2 * EH]).then_inc(s["b_ready"], 1)
            dve.wait_ge(s["slot_hi"], 1)
            dve.tensor_tensor(seT[1][:], se_T, seT[0][:].bitcast(F32), ALU.subtract).then_inc(s["slot_lo"], 1)
            dve.wait_ge(s["split_hi"], 1)
            dve.tensor_tensor(wg[1][:], wg_raw, wg[0][:].bitcast(F32), ALU.subtract).then_inc(s["split_lo"], 1)
            dve.wait_ge(s["split_hi"], 2)
            dve.tensor_tensor(wu[1][:], wu_raw, wu[0][:].bitcast(F32), ALU.subtract).then_inc(s["split_lo"], 1)
            dve.wait_ge(s["split_lo"], 2)
            dve.wait_ge(s["wd_loaded"], 32)

            def hidden(k, e, ch, half):
                q = 4 * k + 2 * e + half
                need(dve, s["up"], q + 1)
                need(dve, s["gelu"], q + 1)
                need(dve, s["down"], 2 * k + e - 1)
                dve.scalar_tensor_tensor(hid[e][:, half, :], U[half][:], bcol[:, 1, 4 * ch + 2 * e + half:][:, 0:1],
                                         gel[half][:], ALU.add, ALU.mult).then_inc(s["hidden"], 1)

            def expert_out(k, e, ch):
                need(dve, s["down"], 2 * k + e + 1)
                need(dve, s["combined"], 2 * k + e - 1)
                dve.tensor_tensor(eo[e][:], DN[:], over(bd[:, 2 * ch + e, :], OP, 1), ALU.add
                                  ).then_inc(s["eo_ready"], 1)

            def finish(o, par):
                need(dve, s["combined"], 2 * CH * (o + 1))
                need(dve, s["x_normed"], o + 1)
                for p in range(OP):
                    last = dve.scalar_tensor_tensor(fresh[:, p, :], OUT[:, p, :], ra[par][:, p:p + 1],
                                                    c.x[:, 4 * o + p, :], ALU.mult, ALU.add)
                last.then_inc(s["x_new"], 1)
                keep_fresh(c, dve, o, fresh, bn, s["x_new"], s["bn"])

            def body(o, par):
                for ch in range(CH):
                    k = o * CH + ch
                    if has_core(o):
                        hidden(k, 0, ch, 0)
                        if ch == 0 and not (isinstance(o, int) and o == 0):
                            finish(o - 1, 1 - par)
                    if exists(o, ch, 2):
                        e = eb[ch % 2]
                        need(dve, s["lb"], k + 3)
                        scores = M0.rearrange("p (b n) -> p b n", b=OB)
                        dve.tensor_reduce(nm[:], scores, AX.X, ALU.max, negate=True).then_inc(s["lb_max"], 1)
                        need(dve, s["lb_max"], k + 3)
                        need(dve, s["td"], k + 1)
                        dve.tensor_tensor(e[:], scores, over(nm[:], SEQ, 2), ALU.add).then_inc(s["lb_shifted"], 1)
                    if ch == 0 and has_head(o):
                        need(dve, s["x_normed"], o + 1)
                        for p in range(OP):
                            t = 4 * (o + 1) + p
                            last = dve.tensor_scalar(xh[:, p, :], c.x[:, t, :], c.stats[:, t, 0:1],
                                                     c.inv[:, bass.ds(t, 1)], ALU.subtract, ALU.mult)
                        last.then_inc(s["x_hat"], 1)
                    if has_core(o):
                        hidden(k, 0, ch, 1)
                        hidden(k, 1, ch, 0)
                        expert_out(k, 0, ch)
                        hidden(k, 1, ch, 1)
                    if exists(o, ch, 1):
                        i = (ch + 1) % 2
                        need(dve, s["sl_hi"], k + 2)
                        need(dve, s["up"], 4 * k)
                        for b in range(2):
                            hi, lo = (sl[i][n][:].rearrange("p e (t b) n -> p e t b n", b=2)[:, :, :, b, :] for n in (0, 1))
                            last = dve.tensor_tensor(
                                lo, M[:, b, :].rearrange("p (t e n) -> p e t n", t=OP, e=2), hi.bitcast(F32), ALU.subtract)
                        last.then_inc(s["sl_lo"], 1)
                    if has_core(o):
                        expert_out(k, 1, ch)
                    if ch == 1 and has_head(o):
                        need(dve, s["lnT_hi"], o + 2)
                        need(dve, s["la"], 4 * o)
                        need(dve, s["lb"], 8 * o)
                        t = lnT[1 - par]
                        dve.tensor_tensor(t[1][:], M0, t[0][:].bitcast(F32), ALU.subtract).then_inc(s["lnT_lo"], 1)
                    if 2 <= ch < 2 + OP and has_head(o):
                        p = ch - 2
                        need(dve, s["la"], 4 * (o + 1) + p + 1)
                        need(dve, s["la_exp"], 4 * (o + 1) + p)
                        dve.tensor_reduce(na[:, p:p + 1], M[:].rearrange("p a n -> p (a n)"), AX.X, ALU.max, negate=True
                                          ).then_inc(s["la_max"], 1)
                        if p == OP - 1:
                            need(dve, s["la_exp"], 4 * (o + 2))
                            r = ra[1 - par]
                            dve.reciprocal(r[:], r[:]).then_inc(s["la_inv"], 1)
                            need(dve, s["la_inv"], o + 2)
                            dve.tensor_scalar(r[:], r[:], c.gates[:, 1:2], None, ALU.mult).then_inc(s["la_gated"], 1)
                    if exists(o, ch, 2):
                        e = eb[ch % 2]
                        need(dve, s["lb_exp"], k + 3)
                        need(dve, s["eb_normed"], k + 2)
                        dve.tensor_reduce(rb[:], e[:], AX.X, ALU.add).then_inc(s["lb_sum"], 1)
                        need(dve, s["lb_sum"], k + 3)
                        dve.reciprocal(rb[:], rb[:]).then_inc(s["lb_inv"], 1)

            walk(dve, body)
            finish(OCTETS - 1, 1)

        @block.scalar
        def _(act):
            for n, wide in enumerate((PAIRS, CH)):
                act.wait_ge(s["inv_a"], n + 1)
                act.activation(work[:, n, 0:wide], work[:, n, 0:wide], ACT.Sqrt).then_inc(s["inv_b"], 1)
            act.wait_ge(s["slot_gb"], 1)
            act.wait_ge(s["slot_tx"], 1)
            act.activation(se_T, M[:].rearrange("p a n -> p (a n)"), ACT.Identity, bias=slot_gb[:, 1:2],
                           scale=slot_gb[:, 0:1]).then_inc(s["slot_T"], 1)
            act.wait_ge(s["slot_T"], 1)
            act.copy(seT[0][:], se_T).then_inc(s["slot_hi"], 1)
            act.wait_ge(s["wg_loaded"], 16)
            act.copy(wg[0][:], wg_raw).then_inc(s["split_hi"], 1)
            act.wait_ge(s["wu_loaded"], 16)
            act.copy(wu[0][:], wu_raw).then_inc(s["split_hi"], 1)
            act.wait_ge(s["b_ready"], 1)
            act.wait_ge(s["split_lo"], 2)
            act.wait_ge(s["zeroed"], 4)

            def gelu(k, e, ch, half):
                q = 4 * k + 2 * e + half
                need(act, s["gate"], q + 1)
                need(act, s["hidden"], q - 1)
                act.activation(gel[half][:], G[half][:], ACT.Gelu, bias=bcol[:, 0, 4 * ch + 2 * e + half:][:, 0:1]
                               ).then_inc(s["gelu"], 1)

            def body(o, par):
                for ch in range(CH):
                    k = o * CH + ch
                    i = (ch + 1) % 2
                    if has_core(o):
                        gelu(k, 0, ch, 0)
                        gelu(k, 0, ch, 1)
                    if exists(o, ch, 1):
                        need(act, s["td"], k + 2)
                        need(act, s["sl"], k + 1)
                        act.copy(dn[:], M1).then_inc(s["d_ready"], 1)
                    if has_core(o):
                        gelu(k, 1, ch, 0)
                    if exists(o, ch, 1):
                        need(act, s["ct_t"], k + 2)
                        need(act, s["combined"], 2 * k)
                        for e in range(2):
                            for b in range(2):
                                last = act.copy(ct[i][e][b * SEQ:(b + 1) * SEQ, :, b * SEQ:(b + 1) * SEQ],
                                                M1[e * SEQ:(e + 1) * SEQ, :, b * SEQ:(b + 1) * SEQ])
                        last.then_inc(s["ct_ready"], 1)
                    if has_core(o):
                        gelu(k, 1, ch, 1)
                    if exists(o, ch, 1):
                        need(act, s["sl"], k + 2)
                        need(act, s["up"], 4 * k)
                        need(act, s["sl_lo"], k)
                        for b in range(2):
                            hi = sl[i][0][:].rearrange("p e (t b) n -> p e t b n", b=2)[:, :, :, b, :]
                            last = act.copy(hi, M[:, b, :].rearrange("p (t e n) -> p e t n", t=OP, e=2))
                        last.then_inc(s["sl_hi"], 1)
                    if ch == 1 and has_head(o):
                        need(act, s["tx"], o + 2)
                        need(act, s["la"], 4 * o)
                        need(act, s["lb"], 8 * o)
                        act.copy(lnT[1 - par][0][:], M0).then_inc(s["lnT_hi"], 1)
                    if exists(o, ch, 2):
                        need(act, s["lb_shifted"], k + 3)
                        act.activation(eb[ch % 2][:], eb[ch % 2][:], ACT.Exp).then_inc(s["lb_exp"], 1)
                    if 2 <= ch < 2 + OP and has_head(o):
                        p = ch - 2
                        need(act, s["la_max"], 4 * (o + 1) + p + 1)
                        need(act, s["ct_t"], 8 * o)
                        need(act, s["x_new"], o)
                        act.activation(ca[1 - par][:, p, :], M[:].rearrange("p a n -> p (a n)"), ACT.Exp,
                                       bias=na[:, p:p + 1], accum_out=ra[1 - par][:, p:p + 1]).then_inc(s["la_exp"], 1)

            walk(act, body)

        @block.tensor
        def _(pe):
            pe.wait_ge(s["rows_loaded"], 32)
            for n in range(2):
                last = pe.transpose(DN[:, 0, n * EH:(n + 1) * EH], b_rows[:, n, :], c.ident[0:EH, 0:EH])
            last.then_inc(s["b_t"], 1)
            pe.wait_ge(s["slot_hat"], CH)
            for t in range(CH):
                last = pe.transpose(M[:, t // OP, (t % OP) * P:(t % OP + 1) * P], se_hat[:, t, :], c.ident[:])
            last.then_inc(s["slot_tx"], 1)
            pe.wait_ge(s["slot_lo"], 1)
            pe.wait_ge(s["b_ready"], 1)
            pe.wait_ge(s["split_lo"], 2)
            pe.wait_ge(s["wd_loaded"], 32)

            def gate_up(k, e, ch, half):
                q = 4 * k + 2 * e + half
                need(pe, s["sl_hi"], k + 1)
                need(pe, s["sl_lo"], k + 1)
                x = [sl[ch % 2][n][:, e, :, :].rearrange("p b n -> p (b n)") for n in (0, 1)]
                cols = slice(half * P, (half + 1) * P)
                need(pe, s["gelu"], q - 1)
                product3(pe, G[half][:], [w[:, 2 * ch + e, cols] for w in wg], x).then_inc(s["gate"], 1)
                need(pe, s["hidden"], q - 1)
                product3(pe, U[half][:], [w[:, 2 * ch + e, cols] for w in wu], x).then_inc(s["up"], 1)

            def down(k, e, ch):
                need(pe, s["hidden"], 4 * k + 2 * e + 2)
                need(pe, s["eo_ready"], 2 * k + e)
                for t in range(OP):
                    for half in range(2):
                        last = pe.matmul(DN[:, t, :], hid[e][:, half, t * P:(t + 1) * P], wd[:, 2 * ch + e, half, :],
                                         start=(half == 0), stop=(half == 1))
                last.then_inc(s["down"], 1)

            def combine(k, e, ch, o=None):
                need(pe, s["eo_ready"], 2 * k + e + 1)
                first = ch == 0 and e == 0
                if first:
                    need(pe, s["x_new"], o)
                for t in range(OP):
                    last = pe.matmul(OUT[:, t, :], ct[ch % 2][e][:, t, :], eo[e][:, t, :], start=first and t == 0,
                                     stop=(ch == CH - 1 and e == 1), skip_group_check=True)
                last.then_inc(s["combined"], 1)

            def body(o, par):
                for ch in range(CH):
                    k = o * CH + ch
                    i = (ch + 1) % 2
                    if has_core(o):
                        gate_up(k, 0, ch, 0)
                        if exists(o, ch, -1):
                            combine(k - 1, 1, (ch - 1) % CH)
                    if exists(o, ch, 2):
                        need(pe, s["sl_hi"], k + 1)
                        need(pe, s["sl_lo"], k + 1)
                        if ch == 2 and has_head(o):
                            need(pe, s["lnT_hi"], o + 2)
                            need(pe, s["lnT_lo"], o + 2)
                        if 3 <= ch <= 6 and has_head(o):
                            need(pe, s["la_exp"], 4 * (o + 1) + ch - 2)
                        need(pe, s["lb_shifted"], k + 2)
                        c2 = (ch + 2) % CH
                        ln = lnT[par if ch < CH - 2 else 1 - par]
                        product3(pe, M0, [w[:, c2 * P:(c2 + 1) * P] for w in seT], [w[:] for w in ln]
                                 ).then_inc(s["lb"], 1)
                    if has_core(o):
                        gate_up(k, 0, ch, 1)
                    if exists(o, ch, 1):
                        need(pe, s["eb_normed"], k + 2)
                        need(pe, s["sl_hi"], k + 1)
                        need(pe, s["sl_lo"], k + 1)
                        e = eb[i][:].rearrange("p (t b) n -> p t (b n)", b=2)
                        for t in range(OP):
                            last = pe.transpose(M1[:, t, :], e[:, t, :], c.ident[:])
                        last.then_inc(s["td"], 1)
                    if has_core(o):
                        gate_up(k, 1, ch, 0)
                    if exists(o, ch, 1):
                        need(pe, s["d_ready"], k + 2)
                        src = ca[par if ch < CH - 1 else 1 - par]
                        c1 = (ch + 1) % CH
                        if c1 == 0:
                            need(pe, s["la_exp"], 4 * (o + 2))
                        for t in range(OP):
                            last = pe.transpose(M1[:, t, :], src[:, t, c1 * P:(c1 + 1) * P], c.ident[:])
                        last.then_inc(s["ct_t"], 1)
                    if has_core(o):
                        down(k, 0, ch)
                        gate_up(k, 1, ch, 1)
                    if exists(o, ch, 1):
                        need(pe, s["ct_ready"], k + 2)
                        if exists(o, ch, 2):
                            need(pe, s["lb_shifted"], k + 3)
                        src = xn[par if ch < CH - 1 else 1 - par]
                        for b in range(OB):
                            r = slice((b % 2) * SEQ, (b % 2 + 1) * SEQ)
                            last = pe.matmul(M[:, b % 2, (b // 2) * P:(b // 2 + 1) * P], src[r, b // 2, :],
                                             dn[r, b // 2, :], start=True, stop=True)
                        last.then_inc(s["sl"], 1)
                    if has_core(o):
                        need(pe, s["ct_ready"], k + 1)
                        combine(k, 0, ch, o)
                        down(k, 1, ch)
                    if ch == 1 and has_head(o):
                        need(pe, s["x_normed"], o + 2)
                        need(pe, s["sl_hi"], k + 2)
                        need(pe, s["sl_lo"], k + 2)
                        for t in range(OP):
                            last = pe.transpose(M[:, 0, t * P:(t + 1) * P], xn[1 - par][:, t, :], c.ident[:])
                        last.then_inc(s["tx"], 1)
                    if 2 <= ch < 2 + OP and has_head(o):
                        p = ch - 2
                        need(pe, s["sl_hi"], k + 2)
                        need(pe, s["sl_lo"], k + 2)
                        need(pe, s["lnT_hi"], o + 2)
                        need(pe, s["lnT_lo"], o + 2)
                        need(pe, s["la_exp"], 4 * (o + 1) + p)
                        for half in range(2):
                            last = product3(pe, M[:, half, :], [w[:, p * P:(p + 1) * P] for w in lnT[1 - par]],
                                            [w[:, half * 512:(half + 1) * 512] for w in seT])
                        last.then_inc(s["la"], 1)

            walk(pe, body)
            combine(LAST, 1, CH - 1)


def stage_attention1(c):
    nc, ins = c.nc, c.ins
    H = 8
    HP = H // 2
    SCALE = float(D) ** -0.5
    with ExitStack() as ctx:
        sb, sem = c.sb(ctx), c.sem(ctx)
        ctx_sb = sb("ctx1", [P, PAIRS, D])
        work = sb("inv_work2", [P, 1, PAIRS])
        wq, wkv, wo = sb("w_q1", [P, H, D]), sb("w_kv1", [P, 2 * H, D]), sb("w_o1", [P, H, D])
        wT = [sb(f"w_{n}T1", [P, H, D]) for n in "qkv"]
        a = [sb(f"A_{n}", [P, H, D], F32R) for n in ("hi", "lo")]
        a_raw = sb("A_raw", [P, H, D])
        bh = sb("B", [P, H, D])
        b_rows = sb("b_rows1", [H, 2, D])
        b_cols = sb("b_cols1", [P, 2, H])
        bv_all = sb("bv_all", [P, H, P])
        cq = sb("cq", [P, H])
        bo, gbo = sb("b_o1", [P, D]), sb("gated_b_o1", [P, D])
        cols = sb("norm_cols1", [P, 4])
        xh, ch = sb("x_hat2", [P, OP, D]), sb("ctx_hat2", [P, OP, D])
        kvT = [sb(f"kv_inT{i}", [P, OB, P]) for i in range(2)]
        kvN = [sb(f"kv_in2_{i}", [P, OB, D]) for i in range(2)]
        lat = [sb(f"latents_{n}", [P, OB, SEQ], F32R) for n in ("hi", "lo")]
        qT = [sb(f"qAT{i}", [P, OB, H, SEQ]) for i in range(2)]
        pr = [sb(f"probs1_{i}", [P, HP, P]) for i in range(4)]
        nmax, rs = [sb(f"neg_max1_{i}", [P, HP]) for i in range(2)], sb("row_sum1", [P, HP])
        pT = [sb(f"probsT1_{i}", [P, HP * P]) for i in range(2)]
        yT = [sb(f"yT{i}", [P, H, P]) for i in range(2)]
        fresh, bn = sb("x_fresh2", [P, D]), sb("bn_c", [P, 6])

        S = [c.bank(ctx, f"psS{i}", [P, HP, P]) for i in range(2)]
        X = c.bank(ctx, "psX2", [P, OB, P], 2)
        Q, T = c.bank(ctx, "psQ"), c.bank(ctx, "psT2", [P, HP, P])
        Y, O = c.bank(ctx, "psY"), c.bank(ctx, "psO2")
        WX = [(X[:, 0:HP, :], X[:, HP:H, :]), (S[0][:], S[1][:]), (T[:], Q[:].rearrange("p (h d) -> p h d", h=HP))]

        names = ("w_loaded o_loaded cols_loaded rows_loaded aggr inv_a inv_b inv_done wt wT_ready bt "
                 "b_ready bv_ready a_prod a_raw a_hi a_lo cq_prod cq_ready b_prod bh_ready bo_prod bo_ready gbo_ready "
                 "x_hat ctx_hat tx kvT lat_hi lat_lo kn kvN q q_ready scores neg_max shifted exped row_sum row_inv normed "
                 "tp probsT av yT out x_biased x_new bn x_kept")
        s = {n: sem("c_" + n) for n in names.split()}
        ctx_loaded = [sem(f"c_ctx_loaded{n}") for n in range(4)]
        block = ctx.enter_context(nc.Block())

        def exists(o, j, back):
            return not isinstance(o, int) or 0 <= OB * o + j - back < BATCHES

        def q_bank(o, h):
            return Y if not has_core(o) and h % 2 else Q

        def parity(par, j, back):
            return par if j >= back else 1 - par

        def slots(eng, slot):
            def body(o, par):
                for j in range(OB):
                    slot(o, par, j)
            walk(eng, body)
            for j in range(6):
                slot(OCTETS, 0, j)

        @block.sync
        def _(sp):
            sp.dma_start(b_rows[:, 0, :], ins["L1_xattn_bq"].rearrange("(h d) -> h d", h=H)).then_inc(s["rows_loaded"], 16)
            sp.dma_start(b_rows[:, 1, :], ins["L1_xattn_bkv"][H * D:2 * H * D].rearrange("(h d) -> h d", h=H)
                         ).then_inc(s["rows_loaded"], 16)
            sp.dma_start(wq[:].rearrange("p h d -> p (h d)"), ins["L1_xattn_Wq"]).then_inc(s["w_loaded"], 16)
            sp.dma_start(wkv[:].rearrange("p h d -> p (h d)"), ins["L1_xattn_Wkv"]).then_inc(s["w_loaded"], 16)
            sp.dma_start(wo[:], ins["L1_xattn_Wo"].rearrange("(h k) o -> k h o", k=D)).then_inc(s["o_loaded"], 16)
            sp.dma_start(bo[:], all_rows(ins["L1_xattn_bo"])).then_inc(s["o_loaded"], 16)
            for n, name in enumerate(("gamma_media", "beta_media", "gamma_lat", "beta_lat")):
                sp.dma_start(cols[:, n:n + 1], column(ins["L1_xattn_" + name])).then_inc(s["cols_loaded"], 16)
            for n in range(4):
                r = slice(n * PAIRS // 4, (n + 1) * PAIRS // 4)
                sp.dma_start(ctx_sb[:, r, :], tokens(ins["ctx_1024"])[:, r, :]).then_inc(ctx_loaded[n], 16)

        @block.gpsimd
        def _(pool):
            pool.wait_ge(s["b_ready"], 1)
            pool.tensor_copy(bv_all[:], over(b_cols[:, 1, :], P, 2)).then_inc(s["bv_ready"], 1)
            pool.wait_ge(s["bo_ready"], 1)
            pool.tensor_scalar(gbo[:], bo[:], c.gates[:, 2:3], None, ALU.mult).then_inc(s["gbo_ready"], 1)
            pool.wait_ge(s["gbo_ready"], 1)

            def slot(o, par, j):
                n = o * OB + j
                if exists(o, j, 1):
                    need(pool, s["row_inv"], n)
                    p = pr[(j - 1) % 4]
                    pool.tensor_tensor(p[:], p[:], over(rs[:], P, 2), ALU.mult).then_inc(s["normed"], 1)
                if j == 0 and has_head(o):
                    need(pool, s["x_hat"], o + 2)
                    xo = c.x[:, bass.ds(4 * (o + 1), OP), :]
                    pool.tensor_tensor(xo, xo, over(gbo[:], OP, 1), ALU.add).then_inc(s["x_biased"], 1)
                if j == 1 and has_head(o):
                    need(pool, s["kvT"], 2 * (o + 2))
                    need(pool, s["lat_hi"], o + 2)
                    need(pool, s["q"], 8 * (o + 1))
                    pool.tensor_tensor(lat[1][:], kvT[1 - par][:, :, SEQ:P], lat[0][:].bitcast(F32), ALU.subtract
                                       ).then_inc(s["lat_lo"], 1)

            slots(pool, slot)

        @block.vector
        def _(dve):
            x_stats(c, dve, s["aggr"])
            norm_scales(dve, work, [(c.stats, True)], s["inv_a"])
            dve.wait_ge(s["inv_b"], 1)
            dve.reciprocal(c.inv[:], work[:, 0, :]).then_inc(s["inv_done"], 1)
            dve.wait_ge(s["inv_done"], 1)
            def hats(h):
                need(dve, s["tx"], h)
                for p in range(OP):
                    t = OP * h + p
                    last = dve.tensor_scalar(xh[:, p, :], c.x[:, t, :], c.stats[:, t, 0:1],
                                             c.inv[:, bass.ds(t, 1)], ALU.subtract, ALU.mult)
                last.then_inc(s["x_hat"], 1)
                for p in range(OP):
                    t = OP * h + p
                    last = dve.tensor_scalar(ch[:, p, :], ctx_sb[:, t, :], c.cstats[:, t, 0:1],
                                             c.cinv[:, bass.ds(t, 1)], ALU.subtract, ALU.mult)
                last.then_inc(s["ctx_hat"], 1)

            dve.wait_ge(s["bt"], 1)
            dve.tensor_copy(b_cols[:], O[:, 0:2 * H]).then_inc(s["b_ready"], 1)
            for w in range(3):
                dve.wait_ge(s["wt"], w + 1)
                for n in range(2):
                    dve.tensor_copy(wT[w][:, n * HP:(n + 1) * HP, :], WX[w][n]).then_inc(s["wT_ready"], 1)
            for n in range(4):
                dve.wait_ge(ctx_loaded[n], 16)
            hats(0)
            dve.wait_ge(s["a_prod"], 1)
            dve.tensor_copy(a_raw[:], X[:]).then_inc(s["a_raw"], 1)
            dve.wait_ge(s["cq_prod"], 1)
            dve.tensor_scalar(cq[:], Y[:, 0:H], SCALE, None, ALU.mult).then_inc(s["cq_ready"], 1)
            dve.wait_ge(s["a_hi"], 1)
            dve.tensor_tensor(a[1][:], a_raw[:], a[0][:].bitcast(F32), ALU.subtract).then_inc(s["a_lo"], 1)
            dve.wait_ge(s["b_prod"], 1)
            dve.tensor_copy(bh[:], X[:]).then_inc(s["bh_ready"], 1)
            dve.wait_ge(s["bo_prod"], 1)
            dve.tensor_tensor(bo[:], O[:, 0:D], bo[:], ALU.add).then_inc(s["bo_ready"], 1)

            def slot(o, par, j):
                n = o * OB + j
                if j == 0 and has_head(o) and has_core(o):
                    hats(o + 1)
                if exists(o, j, 0):
                    need(dve, s["scores"], n + 1)
                    dve.tensor_reduce(nmax[j % 2][:], S[j % 2][:], AX.X, ALU.max, negate=True).then_inc(s["neg_max"], 1)
                    need(dve, s["neg_max"], n + 1)
                    need(dve, s["tp"], n - 3)
                    dve.tensor_tensor(pr[j % 4][:], S[j % 2][:], over(nmax[j % 2][:], P, 2), ALU.add).then_inc(s["shifted"], 1)
                if exists(o, j, 1):
                    need(dve, s["exped"], n)
                    need(dve, s["normed"], n - 1)
                    dve.tensor_reduce(rs[:], pr[(j - 1) % 4][:], AX.X, ALU.add).then_inc(s["row_sum"], 1)
                    need(dve, s["row_sum"], n)
                    dve.reciprocal(rs[:], rs[:]).then_inc(s["row_inv"], 1)
                if j % 2 == 1 and exists(o, j, 5):
                    t = 4 * o + (j - 5) // 2
                    need(dve, s["out"], t + 1)
                    need(dve, s["x_biased"], o + (1 if j >= 5 else 0))
                    need(dve, s["x_kept"], t)
                    dve.scalar_tensor_tensor(fresh[:], O[:, 0:D], c.gates[:, 2:3], c.x[:, t, :], ALU.mult, ALU.add
                                             ).then_inc(s["x_new"], 1)
                    need(dve, s["x_new"], t + 1)
                    dve.bn_stats(bn[:], fresh[:]).then_inc(s["bn"], 1)
                    dve.tensor_scalar(c.x[:, t, :], fresh[:], 1.0, None, ALU.mult)
                    need(dve, s["bn"], t + 1)
                    dve.tensor_scalar(c.bn[:, t, :], bn[:], 1.0, None, ALU.mult).then_inc(s["x_kept"], 1)

            slots(dve, slot)

        @block.scalar
        def _(act):
            act.wait_ge(s["inv_a"], 1)
            act.activation(work[:, 0, :], work[:, 0, :], ACT.Sqrt).then_inc(s["inv_b"], 1)
            act.wait_ge(s["a_raw"], 1)
            act.copy(a[0][:], a_raw[:]).then_inc(s["a_hi"], 1)
            act.wait_ge(s["cols_loaded"], 64)
            act.wait_ge(s["cq_ready"], 1)

            def q_out(o, par, h):
                Q = q_bank(o, h)
                need(act, s["q"], 8 * (o + 1) + h + 1)
                need(act, s["scores"], 8 * o)
                act.activation(qT[1 - par][:, :, h, :], Q[:].rearrange("p (b n) -> p b n", b=OB), ACT.Identity,
                               bias=cq[:, h:h + 1], scale=SCALE).then_inc(s["q_ready"], 1)

            def slot(o, par, j):
                n = o * OB + j
                if 2 <= j <= 5 and has_head(o):
                    q_out(o, par, 2 * (j - 2))
                if exists(o, j, 0):
                    need(act, s["shifted"], n + 1)
                    act.activation(pr[j % 4][:], pr[j % 4][:], ACT.Exp).then_inc(s["exped"], 1)
                if exists(o, j, 2):
                    need(act, s["tp"], n - 1)
                    need(act, s["av"], n - 3)
                    act.copy(pT[j % 2][:], T[:].rearrange("p a b -> p (a b)")).then_inc(s["probsT"], 1)
                if 2 <= j <= 5 and has_head(o):
                    q_out(o, par, 2 * (j - 2) + 1)
                if exists(o, j, 3):
                    m = (j - 3) % OB
                    need(act, s["av"], n - 2)
                    need(act, s["out"], 4 * o + (j - 3) // 2 - 1)
                    act.copy(yT[(m // 2) % 2][:, :, (m % 2) * SEQ:(m % 2 + 1) * SEQ],
                             Y[:].rearrange("p (h n) -> p h n", h=H)).then_inc(s["yT"], 1)
                if j == 0 and has_head(o):
                    need(act, s["tx"], o + 2)
                    need(act, s["scores"], 8 * o)
                    act.activation(kvT[1 - par][:, :, SEQ:P], X[:, OP:OB, :].rearrange("p t (b n) -> p (t b) n", b=2),
                                   ACT.Identity, bias=cols[:, 3:4], scale=cols[:, 2:3]).then_inc(s["kvT"], 1)
                    act.activation(kvT[1 - par][:, :, 0:SEQ], X[:, 0:OP, :].rearrange("p t (b n) -> p (t b) n", b=2),
                                   ACT.Identity, bias=cols[:, 1:2], scale=cols[:, 0:1]).then_inc(s["kvT"], 1)
                    need(act, s["q"], 8 * (o + 1))
                    act.activation(lat[0][:], X[:, OP:OB, :].rearrange("p t (b n) -> p (t b) n", b=2),
                                   ACT.Identity, bias=cols[:, 3:4], scale=cols[:, 2:3]).then_inc(s["lat_hi"], 1)
                if j == 2 and has_head(o):
                    need(act, s["kn"], o + 2)
                    need(act, s["av"], 8 * o)
                    act.copy(kvN[1 - par][:], X[:]).then_inc(s["kvN"], 1)

            slots(act, slot)

        @block.tensor
        def _(pe):
            pe.wait_ge(s["rows_loaded"], 32)
            for n in range(2):
                last = pe.transpose(O[:, n * H:(n + 1) * H], b_rows[:, n, :], c.ident[0:H, 0:H])
            last.then_inc(s["bt"], 1)
            pe.wait_ge(s["w_loaded"], 32)
            for w in range(3):
                for h in range(H):
                    src = wq[:, h, :] if w == 0 else wkv[:, (w - 1) * H + h, :]
                    last = pe.transpose(WX[w][h // HP][:, h % HP, :], src, c.ident[:])
                last.then_inc(s["wt"], 1)
            pe.wait_ge(s["wT_ready"], 6)
            for h in range(H):
                last = pe.matmul(X[:, h, :], wT[0][:, h, :], wT[1][:, h, :], start=True, stop=True)
            last.then_inc(s["a_prod"], 1)
            pe.wait_ge(s["b_ready"], 1)
            for h in range(H):
                last = pe.matmul(Y[:, h:h + 1], wT[1][:, h, :], b_cols[:, 0, h:h + 1], start=True, stop=True)
            last.then_inc(s["cq_prod"], 1)
            pe.wait_ge(s["o_loaded"], 32)
            pe.wait_ge(s["bv_ready"], 1)
            for h in range(H):
                last = pe.matmul(O[:, 0:D], bv_all[:, h, :], wo[:, h, :], start=(h == 0), stop=(h == H - 1))
            last.then_inc(s["bo_prod"], 1)
            pe.wait_ge(s["a_raw"], 1)
            for h in range(H):
                last = pe.matmul(X[:, h, :], wT[2][:, h, :], wo[:, h, :], start=True, stop=True)
            last.then_inc(s["b_prod"], 1)
            pe.wait_ge(s["bh_ready"], 1)
            pe.wait_ge(s["bo_ready"], 1)
            pe.wait_ge(s["cq_ready"], 1)
            pe.wait_ge(s["a_lo"], 1)

            def q_in(o, par, h):
                Q = q_bank(o, h)
                need(pe, s["lat_lo"], o + 2)
                need(pe, s["q_ready"], 8 * (o + 1) + h - (not has_core(o)))
                product3(pe, Q[:], [w[:, h, :] for w in a], [w[:].rearrange("p b n -> p (b n)") for w in lat]
                         ).then_inc(s["q"], 1)

            def slot(o, par, j):
                n = o * OB + j
                if exists(o, j, 0):
                    need(pe, s["q_ready"], 8 * (o + 1))
                    need(pe, s["kvT"], 2 * (o + 1))
                    need(pe, s["shifted"], n - 1)
                    for hp in range(HP):
                        last = pe.matmul(S[j % 2][:, hp, :],
                                         qT[par][:, j, 2 * hp:2 * hp + 2, :].rearrange("p h n -> p (h n)"),
                                         kvT[par][:, j, :], start=True, stop=True)
                    last.then_inc(s["scores"], 1)
                if 2 <= j <= 5 and has_head(o):
                    q_in(o, par, 2 * (j - 2))
                if j % 2 == 1 and exists(o, j, 5):
                    m = ((j - 5) % OB) // 2
                    t = 4 * o + (j - 5) // 2
                    need(pe, s["yT"], n - 3)
                    need(pe, s["x_new"], t)
                    for h in range(H):
                        last = pe.matmul(O[:, 0:D], yT[m % 2][:, h, :], bh[:, h, :], start=(h == 0), stop=(h == H - 1))
                    last.then_inc(s["out"], 1)
                if exists(o, j, 2):
                    need(pe, s["normed"], n - 1)
                    need(pe, s["probsT"], n - 2)
                    for hp in range(HP):
                        last = pe.transpose(T[:, hp, :], pr[(j - 2) % 4][:, hp, :], c.ident[:])
                    last.then_inc(s["tp"], 1)
                if 2 <= j <= 5 and has_head(o):
                    q_in(o, par, 2 * (j - 2) + 1)
                if exists(o, j, 3):
                    need(pe, s["probsT"], n - 2)
                    need(pe, s["kvN"], o + (1 if j >= 3 else 0))
                    need(pe, s["yT"], n - 3)
                    pe.matmul(Y[:], kvN[parity(par, j, 3)][:, (j - 3) % OB, :], pT[(j - 3) % 2][:], start=True, stop=True
                              ).then_inc(s["av"], 1)
                if j == 0 and has_head(o):
                    need(pe, s["x_hat"], o + 2)
                    need(pe, s["ctx_hat"], o + 2)
                    need(pe, s["kvN"], o + 1)
                    for p in range(OP):
                        pe.transpose(X[:, p, :], ch[:, p, :], c.ident[:])
                    for p in range(OP):
                        last = pe.transpose(X[:, OP + p, :], xh[:, p, :], c.ident[:])
                    last.then_inc(s["tx"], 1)
                if j == 1 and has_head(o):
                    need(pe, s["kvT"], 2 * (o + 2))
                    need(pe, s["lat_hi"], o + 2)
                    for b in range(OB):
                        last = pe.transpose(X[:, b, :], kvT[1 - par][:, b, :], c.ident[:])
                    last.then_inc(s["kn"], 1)

            slots(pe, slot)


def stage_experts1(c):
    nc, ins = c.nc, c.ins
    E, HALVES = 8, 2
    WB = E * HALVES // OP
    TAKEN = -3e38
    with ExitStack() as ctx:
        sb, sem = c.sb(ctx), c.sem(ctx)
        raw = [sb(f"w_{n}_raw1", [P, E * HALVES, P]) for n in ("gate", "up", "down")]
        wgu = [[sb(f"w_{n}T_{m}1", [P, E * HALVES, P], F32R) for m in ("hi", "lo")] for n in ("gate", "up")]
        wd = sb("w_downT1", [P, E * HALVES, D])
        r_raw = sb("router_raw", [E, D])
        rw = [sb(f"routerT_{m}", [P, E], F32R) for m in ("hi", "lo")]
        work = sb("inv_work3", [P, 1, PAIRS])
        xh = [sb(f"x_hat3_{i}", [P, OP, D]) for i in range(2)]
        lnT = [sb(f"x_normedT3_{m}", [P, OCTETS, OT], F32R) for m in ("hi", "lo")]
        logitsT = [sb(f"logitsT{i}", [E, OT]) for i in range(2)]
        logits, eq = sb("logits", [P, PAIRS, E]), sb("is_max", [P, PAIRS, E])
        taken = [sb(f"taken{i}", [P, PAIRS, E]) for i in range(2)]
        order = sb("order", [P, E])
        top, first = sb("top", [P, 2, PAIRS]), sb("first", [P, PAIRS])
        ratio, share = sb("ratio", [P, PAIRS]), sb("share", [P, 2, PAIRS])
        cw = sb("combine3", [P, PAIRS, E])
        act_ = [sb(f"silu{i}", [P, OT]) for i in range(2)]
        hid = [sb(f"hidden3_{i}", [P, HALVES, OT]) for i in range(2)]

        G = [c.bank(ctx, f"psG3_{i}") for i in range(2)]
        U = [c.bank(ctx, f"psU3_{i}") for i in range(2)]
        Y = [c.bank(ctx, f"psY3_{i}", [P, OP, D]) for i in range(2)]
        TX = [c.bank(ctx, f"psTX3_{i}") for i in range(2)]
        LT = Y[1][0:E].rearrange("p a b -> p (a b)")
        WX = [G[0], U[0], G[1], U[1]]
        L = Y[0][:].rearrange("p a b -> p (a b)")[:, 0:PAIRS * E].rearrange("p (t e) -> p t e", e=E)

        names = ("router_loaded order_ready aggr inv_a inv_b inv_done rt r_hi r_lo wt w_hi w_lo wd_ready x_hat tx "
                 "ln_hi ln_lo lT lT_copied logits copied route ratio cw_ready gate up silu hidden down added")
        s = {n: sem("d_" + n) for n in names.split()}
        w_loaded = [sem(f"d_w_loaded{n}") for n in range(3)]
        block = ctx.enter_context(nc.Block())

        def octets(eng, body):
            body(0)
            with eng.Fori(1, OCTETS) as o:
                body(o)

        @block.sync
        def _(sp):
            sp.dma_start(r_raw[:], ins["L1_ffn_router_w"]).then_inc(s["router_loaded"], 16)
            for n, name in enumerate(("w_gate", "w_up")):
                sp.dma_start(raw[n][:], ins["L1_ffn_" + name].rearrange("e (h f) d -> f (e h) d", h=HALVES)
                             ).then_inc(w_loaded[n], 16)
            sp.dma_start(raw[2][:].rearrange("o (e h) f -> o e (h f)", h=HALVES),
                         ins["L1_ffn_w_down"].rearrange("e o f -> o e f")).then_inc(w_loaded[2], 16)

            def body(o):
                need(sp, s["added"], E * (o + 1))
                sp.dma_start(tokens(c.out)[:, bass.ds(4 * o, OP), :], c.x[:, bass.ds(4 * o, OP), :]
                             ).then_inc(c.stored, 16)

            octets(sp, body)
            sp.wait_ge(c.stored, 16 * OCTETS)

        @block.gpsimd
        def _(pool):
            for e in range(E):
                pool.memset(order[:, e:e + 1], float(E - e)).then_inc(s["order_ready"], 1)

        @block.vector
        def _(dve):
            x_stats(c, dve, s["aggr"])
            norm_scales(dve, work, [(c.stats, False)], s["inv_a"])
            dve.wait_ge(s["inv_b"], 1)
            dve.reciprocal(c.inv[:], work[:, 0, :]).then_inc(s["inv_done"], 1)
            dve.wait_ge(s["inv_done"], 1)
            dve.wait_ge(s["r_hi"], 1)
            dve.tensor_tensor(rw[1][:], Y[1][:, 0, 0:E], rw[0][:].bitcast(F32), ALU.subtract).then_inc(s["r_lo"], 1)

            def x_hat(o):
                need(dve, s["tx"], o - 1)
                for p in range(OP):
                    t = OP * o + p
                    last = dve.tensor_scalar(xh[o % 2][:, p, :], c.x[:, t, :], c.stats[:, t, 0:1], c.inv[:, t:t + 1],
                                             ALU.subtract, ALU.mult)
                last.then_inc(s["x_hat"], 1)

            def weight_lo(k):
                dve.wait_ge(s["w_hi"], k + 1)
                r = slice(k % WB * OP, (k % WB + 1) * OP)
                dve.tensor_tensor(wgu[k // WB][1][:, r, :], WX[k % 4][:].rearrange("p (a b) -> p a b", b=P),
                                  wgu[k // WB][0][:, r, :].bitcast(F32), ALU.subtract).then_inc(s["w_lo"], 1)

            x_hat(0)
            for o in range(OCTETS):
                if o + 1 < OCTETS:
                    x_hat(o + 1)
                dve.wait_ge(s["ln_hi"], o + 1)
                dve.tensor_tensor(lnT[1][:, o, :], TX[o % 2][:], lnT[0][:, o, :].bitcast(F32), ALU.subtract
                                  ).then_inc(s["ln_lo"], 1)
            for k in range(2 * WB):
                weight_lo(k)

            route = 0
            dve.wait_ge(s["logits"], OCTETS)
            dve.tensor_copy(logits[:], L).then_inc(s["copied"], 1)
            dve.wait_ge(s["copied"], 1)
            dve.wait_ge(s["order_ready"], E)
            for k in range(2):
                dve.tensor_reduce(top[:, k, :], logits[:], AX.X, ALU.max).then_inc(s["route"], 1)
                dve.wait_ge(s["route"], route + 1)
                dve.tensor_tensor(eq[:], logits[:], over(top[:, k, :], E, 2), ALU.is_equal).then_inc(s["route"], 1)
                dve.wait_ge(s["route"], route + 2)
                dve.tensor_tensor(eq[:], eq[:], over(order[:], PAIRS, 1), ALU.mult).then_inc(s["route"], 1)
                dve.wait_ge(s["route"], route + 3)
                dve.tensor_reduce(first[:], eq[:], AX.X, ALU.max).then_inc(s["route"], 1)
                dve.wait_ge(s["route"], route + 4)
                dve.tensor_tensor(taken[k][:], eq[:], over(first[:], E, 2), ALU.is_equal).then_inc(s["route"], 1)
                dve.wait_ge(s["route"], route + 5)
                route += 5
                if k == 0:
                    dve.scalar_tensor_tensor(logits[:], taken[0][:], TAKEN, logits[:], ALU.mult, ALU.add
                                             ).then_inc(s["route"], 1)
                    dve.wait_ge(s["route"], route + 1)
                    route += 1
            dve.tensor_tensor(ratio[:], top[:, 1, :], top[:, 0, :], ALU.subtract).then_inc(s["route"], 1)
            dve.wait_ge(s["ratio"], 1)
            dve.tensor_scalar(share[:, 0, :], ratio[:], 1.0, None, ALU.add).then_inc(s["route"], 1)
            dve.wait_ge(s["route"], route + 2)
            dve.reciprocal(share[:, 0, :], share[:, 0, :]).then_inc(s["route"], 1)
            dve.wait_ge(s["route"], route + 3)
            dve.tensor_scalar(share[:, 0, :], share[:, 0, :], c.gates[:, 3:4], None, ALU.mult).then_inc(s["route"], 1)
            dve.wait_ge(s["route"], route + 4)
            dve.tensor_tensor(share[:, 1, :], share[:, 0, :], ratio[:], ALU.mult).then_inc(s["route"], 1)
            dve.wait_ge(s["route"], route + 5)
            for k in range(2):
                dve.tensor_tensor(taken[k][:], taken[k][:], over(share[:, k, :], E, 2), ALU.mult
                                  ).then_inc(s["route"], 1)
            dve.wait_ge(s["route"], route + 7)
            dve.tensor_tensor(cw[:], taken[0][:], taken[1][:], ALU.add).then_inc(s["cw_ready"], 1)
            dve.wait_ge(s["cw_ready"], 1)

            def add(o, e):
                need(dve, s["down"], E * o + e + 1)
                need(dve, s["added"], E * o + e)
                for p in range(OP):
                    t = OP * o + p
                    last = dve.scalar_tensor_tensor(c.x[:, t, :], Y[e % 2][:, p, :], cw[:, t, e:e + 1], c.x[:, t, :],
                                                    ALU.mult, ALU.add)
                last.then_inc(s["added"], 1)

            def body(o):
                for e in range(E):
                    q = 2 * (E * o + e)
                    for half in range(HALVES):
                        need(dve, s["up"], q + half + 1)
                        need(dve, s["silu"], q + half + 1)
                        need(dve, s["down"], E * o + e - 1)
                        dve.tensor_tensor(hid[e % 2][:, half, :], U[half][:], act_[half][:], ALU.mult
                                          ).then_inc(s["hidden"], 1)
                    if e > 0:
                        add(o, e - 1)
                    elif not (isinstance(o, int) and o == 0):
                        add(o - 1, E - 1)

            octets(dve, body)
            add(OCTETS - 1, E - 1)

        @block.scalar
        def _(act):
            act.wait_ge(s["inv_a"], 1)
            act.activation(work[:, 0, :], work[:, 0, :], ACT.Sqrt).then_inc(s["inv_b"], 1)
            act.wait_ge(s["rt"], 1)
            act.copy(rw[0][:], Y[1][:, 0, 0:E]).then_inc(s["r_hi"], 1)

            def logits_out(o):
                act.wait_ge(s["lT"], o + 1)
                need(act, s["logits"], o - 1)
                act.copy(logitsT[o % 2][:], LT).then_inc(s["lT_copied"], 1)

            for o in range(OCTETS):
                act.wait_ge(s["tx"], o + 1)
                act.copy(lnT[0][:, o, :], TX[o % 2][:]).then_inc(s["ln_hi"], 1)
                if o > 0:
                    logits_out(o - 1)
            for k in range(3 * WB):
                act.wait_ge(s["wt"], k + 1)
                r = slice(k % WB * OP, (k % WB + 1) * OP)
                src = WX[k % 4][:].rearrange("p (a b) -> p a b", b=P)
                if k == 1:
                    logits_out(OCTETS - 1)
                if k < 2 * WB:
                    act.copy(wgu[k // WB][0][:, r, :], src).then_inc(s["w_hi"], 1)
                else:
                    act.copy(wd[:, r, :], src).then_inc(s["wd_ready"], 1)
            act.wait_ge(s["route"], 12)
            act.activation(ratio[:], ratio[:], ACT.Exp).then_inc(s["ratio"], 1)

            def body(o):
                for e in range(E):
                    q = 2 * (E * o + e)
                    for half in range(HALVES):
                        need(act, s["gate"], q + half + 1)
                        need(act, s["hidden"], q + half - 1)
                        act.activation(act_[half][:], G[half][:], ACT.Silu).then_inc(s["silu"], 1)

            octets(act, body)

        @block.tensor
        def _(pe):
            pe.wait_ge(s["router_loaded"], 16)
            pe.transpose(Y[1][:, 0, 0:E], r_raw[:], c.ident[0:E, 0:E]).then_inc(s["rt"], 1)

            def router(o):
                pe.wait_ge(s["ln_hi"], o + 1)
                pe.wait_ge(s["ln_lo"], o + 1)
                need(pe, s["lT_copied"], o)
                for n, (a, b) in enumerate(((1, 1), (1, 0), (0, 1), (0, 0))):
                    last = pe.matmul(LT, rw[a][:], lnT[b][:, o, :], start=(n == 0), stop=(n == 3))
                last.then_inc(s["lT"], 1)

            def router_turned(o):
                pe.wait_ge(s["lT_copied"], o + 1)
                for p in range(OP):
                    last = pe.transpose(L[:, OP * o + p, :], logitsT[o % 2][:, p * P:(p + 1) * P], c.ident[0:E, 0:E])
                last.then_inc(s["logits"], 1)

            for o in range(OCTETS):
                pe.wait_ge(s["x_hat"], o + 1)
                need(pe, s["ln_lo"], o - 1)
                for p in range(OP):
                    last = pe.transpose(TX[o % 2][:, p * P:(p + 1) * P], xh[o % 2][:, p, :], c.ident[:])
                last.then_inc(s["tx"], 1)
                if o == 0:
                    pe.wait_ge(s["r_lo"], 1)
                else:
                    router(o - 1)
                if o > 1:
                    router_turned(o - 2)
            for k in range(3 * WB):
                if k % WB == 0:
                    pe.wait_ge(w_loaded[k // WB], 16)
                need(pe, s["w_hi"], k - 3)
                need(pe, s["w_lo"], k - 3)
                for p in range(OP):
                    last = pe.transpose(WX[k % 4][:, p * P:(p + 1) * P], raw[k // WB][:, k % WB * OP + p, :], c.ident[:])
                last.then_inc(s["wt"], 1)
                if k == 0:
                    router(OCTETS - 1)
                    router_turned(OCTETS - 2)
                if k == 1:
                    router_turned(OCTETS - 1)
            pe.wait_ge(s["w_hi"], 2 * WB)
            pe.wait_ge(s["w_lo"], 2 * WB)
            pe.wait_ge(s["wd_ready"], WB)

            def down(o, e):
                q = E * o + e
                need(pe, s["hidden"], 2 * (q + 1))
                if isinstance(o, int) and q < 2:
                    pe.wait_ge(s["copied"], 1)
                need(pe, s["added"], q - 1)
                for t in range(OP):
                    for half in range(HALVES):
                        last = pe.matmul(Y[e % 2][:, t, :], hid[e % 2][:, half, t * P:(t + 1) * P],
                                         wd[:, HALVES * e + half, :], start=(half == 0), stop=(half == 1))
                last.then_inc(s["down"], 1)

            def body(o):
                for e in range(E):
                    q = 2 * (E * o + e)
                    x = [w[:, o, :] for w in lnT]
                    for half in range(HALVES):
                        need(pe, s["silu"], q + half - 1)
                        product3(pe, G[half][:], [w[:, HALVES * e + half, :] for w in wgu[0]], x
                                 ).then_inc(s["gate"], 1)
                        need(pe, s["hidden"], q + half - 1)
                        product3(pe, U[half][:], [w[:, HALVES * e + half, :] for w in wgu[1]], x
                                 ).then_inc(s["up"], 1)
                    if e > 0:
                        down(o, e - 1)
                    elif not (isinstance(o, int) and o == 0):
                        down(o - 1, E - 1)

            octets(pe, body)
            down(OCTETS - 1, E - 1)


def keep_fresh(c, dve, o, fresh, bn, made, bn_done):
    need(dve, made, o + 1)
    for p in range(OP):
        dve.bn_stats(bn[:, p, :], fresh[:, p, :]).then_inc(bn_done, 1)
    dve.tensor_scalar(c.x[:, bass.ds(4 * o, OP), :], fresh[:], 1.0, None, ALU.mult)
    need(dve, bn_done, 4 * o + 4)
    dve.tensor_scalar(c.bn[:, bass.ds(4 * o, OP), :], bn[:], 1.0, None, ALU.mult)


def x_stats(c, dve, done):
    for t in range(PAIRS):
        dve.bn_aggr(c.stats[:, t, :], c.bn[:, t, :]).then_inc(done, 1)
    dve.wait_ge(done, PAIRS)


def norm_scales(dve, work, sources, done):
    for n, (stats, twice) in enumerate(sources):
        a, b = (1.0 + EPS, EPS * EPS) if twice else (1.0, EPS)
        dve.tensor_scalar(work[:, n, 0:stats.shape[1]], stats[:, :, 1], a, b, ALU.mult, ALU.add).then_inc(done, 1)


def program(nc, ins, out, stages=(stage_start, stage_attention0, stage_experts0, stage_attention1, stage_experts1)):
    with ExitStack() as keep:
        c = Chip(nc, ins, out, keep)
        for stage in stages:
            stage(c)


def kernel(**inputs):
    import numpy as np
    from concourse import bacc
    from concourse.bass_utils import run_bass_kernel_spmd

    nc = bacc.Bacc("TRN2", target_bir_lowering=False, num_devices=1)
    arrays, ins = {}, {}
    for name, value in inputs.items():
        a = np.ascontiguousarray(value)
        arrays[f"in_{name}"] = a
        ins[name] = nc.dram_tensor(f"in_{name}", a.shape, mybir.dt.from_np(a.dtype), kind="ExternalInput").ap()
    out = nc.dram_tensor("out", (BATCHES, SEQ, D), F32, kind="ExternalOutput").ap()
    program(nc, ins, out)
    r = run_bass_kernel_spmd(nc, [arrays], core_ids=[0])
    return r.results[0]["out"]
```
